# Optimizing a Trainium2 kernel written in Bass

```python
import numpy as np
import jax
import jax.numpy as jnp

def _softmax(x, axis=-1):
    return jax.nn.softmax(x, axis=axis)

def _gelu(x):
    return jax.nn.gelu(x, approximate=True)

def _silu(x):
    return jax.nn.silu(x)

def _sigmoid(x):
    return jax.nn.sigmoid(x)

def _layernorm(x, axis=-1, eps=1e-05):
    m = jnp.mean(x, axis=axis, keepdims=True)
    v = jnp.var(x, axis=axis, keepdims=True)
    return (x - m) / jnp.sqrt(v + eps)

def _scatter_add(tgt, idx, src, axis=0):
    return tgt.at[idx].add(src)

def _segment_sum(src, seg, n):
    return jax.ops.segment_sum(src, seg, n)
kernel_name = 'mk_flamingo_gated_d1_seqx_r4_f4dd78'

def setup_inputs(seed: int=0):
    np.random.seed(seed)
    _w = jnp.asarray

    def _rec_inputs():
        import jax
        import jax.numpy as jnp
        _rk = jax.random.key(seed)
        x = 7.22e-05 + 1 * jax.random.normal(jax.random.fold_in(_rk, 1), (8, 256, 512), jnp.float32)
        _lenS = 256 - jax.random.randint(jax.random.fold_in(_rk, 7), (8,), 0, max(1, 256 // 4) + 1, jnp.int32)
        _lenS2 = 256 - jax.random.randint(jax.random.fold_in(_rk, 8), (8,), 0, max(1, 256 // 4) + 1, jnp.int32)
        _ctx_512P = jax.random.normal(jax.random.fold_in(_rk, 11), (8, 16, 128), jnp.float32)
        _ctx_512c = jax.random.dirichlet(jax.random.fold_in(_rk, 511), 0.3 * jnp.ones((16,), jnp.float32), (8, 256))
        _ctx_512t = jnp.einsum('bsk,bkd->bsd', _ctx_512c, _ctx_512P)
        _ctx_512t = _ctx_512t * jax.lax.rsqrt(jnp.mean(jnp.square(_ctx_512t)) + 1e-12) * 0.953939
        ctx_512 = -0.000514642 + 1.00011 * (_ctx_512t + 0.3 * jax.random.normal(jax.random.fold_in(_rk, 611), (8, 256, 128), jnp.float32))
        _g = jax.random.normal(jax.random.fold_in(_rk, 9001), (2, 1), jnp.float32)
        _g = jnp.sign(_g) * jnp.maximum(jnp.abs(_g), 1.0) + (_g == 0) * 1.0
        g_xattn = _g[0]
        g_ffn = _g[1]
        return (x, ctx_512, g_xattn, g_ffn)
    x, ctx_512, g_xattn, g_ffn = _rec_inputs()

    def _L0_xattn_setup():
        import jax, jax.numpy as jnp
        import numpy as np
        import math
        NUM_Q_HEADS = 32
        NUM_KV_HEADS = 8
        key = jax.random.key(seed)
        k1, k2, k3 = jax.random.split(key, 3)
        B, S, E = (2, 512, 512)
        kv_E = NUM_KV_HEADS * (E // NUM_Q_HEADS)
        q = jax.random.normal(k1, (B, S, E), dtype=jnp.float32)
        k = jax.random.normal(k2, (B, S, kv_E), dtype=jnp.float32)
        v = jax.random.normal(k3, (B, S, kv_E), dtype=jnp.float32)
        return {'q': q, 'k': k, 'v': v}
    _L0_xattn_all = _L0_xattn_setup()
    _L0_xattn_in = {k: v for k, v in _L0_xattn_all.items() if k in ()}
    del _L0_xattn_all

    def _L0_ffn_setup():
        import jax, jax.numpy as jnp
        import numpy as np
        B, S, H, E, K, I = (2, 256, 512, 32, 8, 192)
        key = jax.random.key(seed)
        ks = jax.random.split(key, 5)
        scaled = lambda k, shp, fan: jax.random.normal(k, shp, jnp.float32) * fan ** (-0.5)
        return {'hidden_states': jax.random.normal(ks[0], (B, S, H), jnp.float32), 'router_w': scaled(ks[1], (E, H), H), 'w_gate': scaled(ks[2], (E, H, I), H), 'w_up': scaled(ks[3], (E, H, I), H), 'w_down': scaled(ks[4], (E, I, H), I)}
    _L0_ffn_all = _L0_ffn_setup()
    _L0_ffn_in = {k: v for k, v in _L0_ffn_all.items() if k in ('router_w', 'w_gate', 'w_up', 'w_down')}
    del _L0_ffn_all
    return {'x': x, 'ctx_512': ctx_512, 'g_xattn': g_xattn, 'g_ffn': g_ffn, 'L0_ffn_router_w': _L0_ffn_in['router_w'], 'L0_ffn_w_gate': _L0_ffn_in['w_gate'], 'L0_ffn_w_up': _L0_ffn_in['w_up'], 'L0_ffn_w_down': _L0_ffn_in['w_down']}

def reference(x, ctx_512, g_xattn, g_ffn, L0_ffn_router_w, L0_ffn_w_gate, L0_ffn_w_up, L0_ffn_w_down):
    import jax
    import jax.numpy as jnp

    def _L0_xattn_ref(q, k, v):
        import jax, jax.numpy as jnp
        import numpy as np
        import math
        NUM_Q_HEADS = 32
        NUM_KV_HEADS = 8
        B, S, E = q.shape
        H, KV = (NUM_Q_HEADS, NUM_KV_HEADS)
        D = E // H
        G = H // KV
        scale = math.sqrt(D)
        qh = q.reshape(B, S, KV, G, D).transpose(0, 2, 3, 1, 4)
        kh = k.reshape(B, S, KV, D).transpose(0, 2, 1, 3)
        vh = v.reshape(B, S, KV, D).transpose(0, 2, 1, 3)
        scores = jnp.einsum('bkgsd,bktd->bkgst', qh, kh) / scale
        weights = jax.nn.softmax(scores, axis=-1)
        out = jnp.einsum('bkgst,bktd->bkgsd', weights, vh)
        return out.transpose(0, 3, 1, 2, 4).reshape(B, S, E)

    def _L0_ffn_ref(hidden_states, router_w, w_gate, w_up, w_down):
        import jax, jax.numpy as jnp
        import numpy as np
        B, S, H, E, K, I = (2, 256, 512, 32, 8, 192)
        Bq, Sq, Hd = hidden_states.shape
        x = hidden_states.reshape(-1, Hd)
        logits = x @ router_w.T
        probs = jax.nn.softmax(logits.astype(jnp.float32), axis=-1)
        rw, sel = jax.lax.top_k(probs, K)
        rw = rw / jnp.sum(rw, axis=-1, keepdims=True)
        rw = rw.astype(x.dtype)

        def body(acc, operand):
            e, wg, wu, wd = operand
            w_e = jnp.sum(jnp.where(sel == e, rw, jnp.zeros_like(rw)), axis=-1)
            h = jax.nn.silu(x @ wg) * (x @ wu)
            return (acc + h @ wd * w_e[:, None], None)
        acc0 = jnp.zeros_like(x)
        acc, _ = jax.lax.scan(body, acc0, (jnp.arange(E), w_gate, w_up, w_down))
        return acc.reshape(Bq, Sq, Hd)
    x = x + jnp.tanh(g_xattn[0]) * _L0_xattn_ref(_layernorm(x, axis=-1), ctx_512, ctx_512)
    x = x + jnp.tanh(g_ffn[0]) * _L0_ffn_ref(_layernorm(x, axis=-1), L0_ffn_router_w, L0_ffn_w_gate, L0_ffn_w_up, L0_ffn_w_down)
    return x

_drawn_inputs = setup_inputs


def setup_inputs(seed=0):
    import zlib

    import numpy as np

    out = dict(_drawn_inputs(seed))
    spreads = {}
    factors = {}
    for name, (base, spread) in spreads.items():
        noise = np.random.default_rng([zlib.crc32(name.encode()), seed]).standard_normal(out[name].shape)
        drawn = base * np.exp(spread * noise) if base else spread * noise
        out[name] = jnp.asarray(drawn.astype(out[name].dtype))
    for name, factor in factors.items():
        out[name] = (out[name] * factor).astype(out[name].dtype)
    return out
```

```python
from contextlib import ExitStack

import concourse.bass as bass
from concourse import mybir

F32 = mybir.dt.float32
F32R = mybir.dt.float32r
BF16 = mybir.dt.bfloat16
I32 = mybir.dt.int32
U32 = mybir.dt.uint32
ALU = mybir.AluOpType
ACT = mybir.ActivationFunctionType
AX = mybir.AxisListType

P = 128
HEADS, KV_HEADS = 32, 8
TOP_K = 8
EPS = 1e-5
ROOT_BITS = float(0x5F3759DF)
NEWTON = 4


def flamingo_block(nc, x, ctx, g_xattn, g_ffn, router_w, w_gate, w_up, w_down, out):
    B, S, D = x.shape
    E, _, I = w_gate.shape
    DH = D // HEADS
    G = HEADS // KV_HEADS
    SC = S // P
    DC = D // P
    T = B * S
    SPARE = T
    ROWS = T + P
    XW = D + E
    PLACES = T // P
    COLS = E * PLACES
    IH = I // 2
    GU_W, WD_W = DC * 2 * I, 2 * D
    STK = 4 * DH
    PAIRS = HEADS // 2
    MAX_TILES = T * TOP_K // P + E
    P_BITS, COL_BITS = P.bit_length() - 1, COLS.bit_length() - 1
    assert D == 512 and SC == 2 and B == 8 and STK == 64 and G == 4 and E == 32

    with ExitStack() as stack:
        def sb(name, shape, dt=F32):
            return stack.enter_context(nc.sbuf_tensor(name, shape, dt))

        def psum(name, shape):
            return stack.enter_context(nc.psum_tensor(name, shape, F32))

        def sem(name):
            return stack.enter_context(nc.semaphore(name))

        def two(make, name, *args):
            return [make(f"{name}{i}", *args) for i in range(2)]

        rows_d = nc.dram_tensor("expert_rows", [ROWS, XW], F32, kind="Internal").ap()
        places_d = nc.dram_tensor("places", [P * COLS, 1], I32, kind="Internal").ap()
        acc_d = [nc.dram_tensor(f"acc{i}", [ROWS, D], F32, kind="Internal").ap() for i in range(2)]

        ident = sb("ident", [P, P])
        ident_r = sb("ident_r", [P, P], F32R)
        earlier = sb("earlier", [P, P], BF16)
        ones = sb("ones", [P, P], BF16)
        zeros = sb("zeros", [P, XW])
        col_base = sb("col_base", [P, SC, E])
        tile_no = sb("tile_no", [P, 2])
        expert_no = sb("expert_no", [P, E])
        gates = sb("gates", [P, 2])
        gates_in = sb("gates_in", [P, 2])
        router_sb = sb("router_sb", [E, D])
        router_T = sb("router_T", [P, DC, E])

        x_in = two(sb, "x_in", [P, SC, D])
        ctx_in = two(sb, "ctx_in", [P, SC, KV_HEADS * DH])
        x_res = two(sb, "x_res", [P, SC, D])
        stats = sb("stats", [P, SC, 6])
        mean_var = sb("mean_var", [P, SC, 2])
        rstd = sb("rstd", [P, SC])
        var_eps = sb("var_eps", [P, SC]); var_half = sb("var_half", [P, SC]); root_sq = sb("root_sq", [P, SC])
        half_bits = sb("half_bits", [P, SC], I32)
        xn = sb("xn", [P, SC, D])
        k_scaled = sb("k_scaled", [P, SC, KV_HEADS * DH])
        q_stage = sb("q_stage", [P, SC, HEADS * STK], F32R)
        k_stage = sb("k_stage", [P, SC, STK + KV_HEADS * 2 * STK], F32R)
        v_aug = two(sb, "v_aug", [P, SC, KV_HEADS, 32])
        qT = two(sb, "qT", [P, PAIRS, S], F32R)
        kT = two(sb, "kT", [P, KV_HEADS, 2, S], F32R)
        maxima = sb("maxima", [P, SC, HEADS])
        max_parts = sb("max_parts", [P, SC, 2 * HEADS], F32R)
        maxT = sb("maxT", [2 * HEADS, S], F32R)
        probs = two(sb, "probs", [P, SC, G * S])
        oT = two(sb, "oT", [P, S])
        recip = sb("recip", [P, 4 * G])
        attn = sb("attn", [P, SC, D])
        x1 = two(sb, "x1", [P, SC, D])
        rows_sb = two(sb, "rows_sb", [P, SC, XW])
        xnT = sb("xnT", [P, SC, D])
        logits = sb("logits", [P, SC, E])
        expd = sb("expd", [P, SC, E])
        row2 = sb("row2", [P, 4, SC])
        pr = sb("pr", [P, SC, E])
        top = sb("top", [P, SC, TOP_K])
        zapped = sb("zapped", [P, SC, E])
        mask = sb("mask", [P, SC, E])
        mask_bf = sb("mask_bf", [P, SC, E], BF16)
        weighted = sb("weighted", [P, SC, E])
        counts = sb("counts", [P, E])
        rank = sb("rank", [P, SC, E])
        rank_i = sb("rank_i", [P, SC, E], I32)
        in_tile = sb("in_tile", [P, SC, E], I32)
        key = sb("key", [P, SC, E])
        place = two(sb, "place", [P, SC * TOP_K], I32)
        token = sb("token", [P, SC])
        token_i = two(sb, "token_i", [P, SC], I32)

        n_tiles = sb("n_tiles", [P, E])
        tile_end = sb("tile_end", [P, E])
        started = sb("started", [P, E])
        whole = sb("whole", [P, E], I32)
        tile_vals = sb("tile_vals", [P, 2, 4])
        lists = sb("lists", [1, 512 + E + 1], I32)
        LIST_E, LIST_END, LIST_PAIRS = 256, 512, 512 + E
        token_of = sb("token_of", [P, COLS + 1], I32)
        gather_idx = two(sb, "gather_idx", [P, 1], I32)
        add_idx = two(sb, "add_idx", [P, 1], I32)
        xg = [x_in[i][:, :, :].rearrange("p c d -> p (c d)")[:, 0:XW] for i in range(2)]
        w_tok = two(sb, "w_tok", [P, 1])
        xT = sb("xT", [P, D])
        silu_g = two(sb, "silu_g", [P, I])
        h = two(sb, "h", [P, I])
        hT = sb("hT", [IH, 2 * P])
        y = two(sb, "y", [P, D])
        w_gu = sb("w_gu", [P, 2 * GU_W])
        w_dn = sb("w_dn", [IH, 2 * WD_W])

        s_max = two(psum, "s_max", [P, 2 * S])
        s_exp = two(psum, "s_exp", [P, G * S])
        o_ps = psum("o_ps", [P, 512])
        t_ps = psum("t_ps", [P, 512])
        t_psr = t_ps[:, :].bitcast(F32R)
        gu_ps, hT_ps, xT_ps = s_max, o_ps, t_ps
        y_ps = [s_exp[i][:, 0:D] for i in range(2)]

        PIECES = 8
        PIECE = T * D // P // PIECES

        def addend(a, n):
            if a == 0 and n < 3:
                return w_gu[:, n * PIECE:(n + 1) * PIECE]
            if a == 1 and n < 4:
                return probs[n // 2][:, n % 2, :]
            t = (x_in[0], x_in[1], attn, xn, xnT)[n - 3] if a == 0 else (x_res + x1)[n - 4]
            return t[:, :, :].rearrange("p c d -> p (c d)")

        consts = sem("consts"); consts_in = sem("consts_in"); scratch_in = sem("scratch_in")
        gates_ready = sem("gates_ready")
        x_loaded = two(sem, "x_loaded"); res_loaded = two(sem, "res_loaded")
        xn_ready = sem("xn_ready"); staged = sem("staged"); pool_step = sem("pool_step")
        dve_step = sem("dve_step"); pe_hold = sem("pe_hold"); place_free = sem("place_free")
        t_full = sem("t_full"); t_free = sem("t_free")
        smax_full = sem("smax_full"); smax_free = sem("smax_free")
        sexp_full = sem("sexp_full"); sexp_free = sem("sexp_free")
        o_full = sem("o_full"); o_free = sem("o_free")
        max_ready = sem("max_ready"); max_rows = sem("max_rows")
        x1_ready = sem("x1_ready"); rows_ready = sem("rows_ready"); w_rows = sem("w_rows")
        x1_stored = two(sem, "x1_stored"); rows_stored = two(sem, "rows_stored")
        shifted = sem("shifted"); expd_ready = sem("expd_ready"); mask_ready = sem("mask_ready")
        place_ready = sem("place_ready"); token_sent = sem("token_sent")
        vals_ready = sem("vals_ready"); lists_ps = sem("lists_ps"); lists_ready = sem("lists_ready")
        places_back = sem("places_back")
        w_in = sem("w_in"); w_ready = sem("w_ready")
        x_got = two(sem, "x_got"); y_sent = two(sem, "y_sent")
        xt_full = sem("xt_full"); xt_ready = sem("xt_ready"); wtok_ready = sem("wtok_ready")
        gu_full = sem("gu_full"); silu_ready = sem("silu_ready"); h_ready = sem("h_ready")
        ht_full = sem("ht_full"); ht_ready = sem("ht_ready")
        y_full = sem("y_full"); y_free = sem("y_free"); idx_ready = sem("idx_ready")
        moe_done = sem("moe_done")
        sum_in = [sem(f"sum_in{i}") for i in range(PIECES)]; summed = sem("summed"); out_done = sem("out_done")

        def wait(eng, s, value):
            if not isinstance(value, int) or value > 0:
                eng.wait_ge(s, value)

        def hold(eng, s):
            eng.sem_inc(s, 1)

        def uses_of_round(first, last, tail_only=False):
            order = []
            if not tail_only:
                for j in range(KV_HEADS):
                    if not last:
                        order += [("Q", j), ("K", j)]
                    if j and j % 2 == 0:
                        order.append(("O", j - 2))
                    if not first:
                        order += {2: [("X", 0)], 3: [("X", 1)], 4: [("L", 0)], 6: [("R", 0)]}.get(j, [])
                order.append(("O", KV_HEADS - 2))
                if not last:
                    order.append(("M", 0))
            else:
                order = [("X", 0), ("X", 1), ("L", 0), ("R", 0)]
            return {u: n for n, u in enumerate(order)}

        T_START = DC
        T_PRE = T_START + 2 * KV_HEADS + 1
        U_FIRST = uses_of_round(True, False)
        U_MID = uses_of_round(False, False)
        U_LAST = uses_of_round(False, True)
        U_TAIL = uses_of_round(False, False, True)
        N_FIRST, N_MID, N_LAST = len(U_FIRST), len(U_MID), len(U_LAST)

        class Round:

            def __init__(self, b, q, m=None):
                self.b, self.q = b, q
                self.m = m if m is not None else b // 2
                self.first = isinstance(b, int) and b == 0
                self.last = isinstance(b, int) and b == B - 1
                self.tail_only = isinstance(b, int) and b == B
                self.uses = U_FIRST if self.first else U_LAST if self.last else U_TAIL if self.tail_only else U_MID
                if self.first:
                    self.t0 = T_PRE
                elif self.tail_only:
                    self.t0 = T_PRE + N_FIRST + (B - 2) * N_MID + N_LAST
                else:
                    self.t0 = (b - 1) * N_MID + (T_PRE + N_FIRST)

            def t(self, kind, j=0):
                return self.t0 + self.uses[(kind, j)]

        def rounds(eng, body):
            body(Round(0, 0))
            with eng.Fori(0, (B - 2) // 2) as n:
                body(Round(2 * n + 1, 1, n))
                body(Round(2 * n + 2, 0, n + 1))
            body(Round(B - 1, (B - 1) % 2))
            body(Round(B, B % 2))

        batch_rows = "(c p) d -> p c d"
        block = stack.enter_context(nc.Block())

        @block.sync
        def _(sp):
            def cut(t, b, n):
                return t[bass.ds(b * S, n * S), :] if not isinstance(b, int) else t[b * S:(b + n) * S, :]

            xf = x.rearrange("b s d -> (b s) d")
            cf = ctx.rearrange("b s d -> (b s) d")

            def load_x(b, q):
                sp.dma_start(x_in[q][:, :, :], cut(xf, b, 1).rearrange(batch_rows, p=P)).then_inc(x_loaded[q], 16)
                sp.dma_start(ctx_in[q][:, :, :], cut(cf, b, 1).rearrange(batch_rows, p=P)).then_inc(x_loaded[q], 16)

            def load_res(b, q):
                sp.dma_start(x_res[q][:, :, :], cut(xf, b, 1).rearrange(batch_rows, p=P)).then_inc(res_loaded[q], 16)

            def insert_max(b, q):
                wait(sp, t_free, b)
                for half in range(2):
                    for part in range(2):
                        at = STK * half + 3 * DH + part
                        sp.dma_start(qT[q][at:at + 1, :, :].bitcast(F32),
                                     maxT[HEADS * part + half:HEADS * (part + 1):2, :].bitcast(F32)).then_inc(max_rows, 16)

            load_x(0, 0)
            sp.dma_start(router_sb[:, :], router_w).then_inc(consts_in, 16)
            sp.dma_start(gates_in[:, 0:1], g_xattn.partition_broadcast(P)).then_inc(consts_in, 16)
            sp.dma_start(gates_in[:, 1:2], g_ffn.partition_broadcast(P)).then_inc(consts_in, 16)
            load_x(1, 1)
            load_res(0, 0)
            sp.wait_ge(consts, 8)
            sp.dma_start(places_d.rearrange("(p c) o -> p (c o)", p=P), token_of[:, 0:COLS]).then_inc(scratch_in, 16)
            for n in range(T // P):
                filled = (x1_stored + rows_stored)[n] if n < 4 else scratch_in
                sp.dma_start(acc_d[1][n * P:(n + 1) * P, :], zeros[:, 0:D]).then_inc(filled, 16)
            insert_max_at = T_PRE
            insert_max(insert_max_at, 0)

            def body(r):
                b, q = r.b, r.q
                if not r.tail_only and not r.last and not (isinstance(b, int) and b + 2 >= B):
                    wait(sp, staged, b + 1)
                    load_x(b + 2, q)
                if not r.first:
                    wait(sp, x1_ready, b)
                    sp.dma_start(cut(acc_d[0], b - 1, 1).rearrange(batch_rows, p=P),
                                 x1[1 - q][:, :, :]).then_inc(x1_stored[1 - q], 16)
                if not r.tail_only and not r.last:
                    load_res(b + 1, 1 - q)
                if not r.first:
                    wait(sp, w_rows, b)
                    sp.dma_start(cut(rows_d, b - 1, 1).rearrange(batch_rows, p=P),
                                 rows_sb[1 - q][:, :, :]).then_inc(rows_stored[1 - q], 16)
                if not r.tail_only and not r.last:
                    insert_max(r.t("M") + 1, 1 - q)

            body(Round(0, 0))
            with sp.Fori(0, (B - 4) // 2) as n:
                body(Round(2 * n + 1, 1, n))
                body(Round(2 * n + 2, 0, n + 1))
            for b in range(B - 3, B + 1):
                body(Round(b, b % 2))

            def load_expert(e, slot):
                one = (slice(e, e + 1) if isinstance(e, int) else bass.ds(e, 1))
                gu = w_gu[:, slot * GU_W:(slot + 1) * GU_W].rearrange("p (c n) -> p c n", c=DC)
                for n, w in enumerate((w_gate, w_up)):
                    sp.dma_start(gu[:, :, n * I:(n + 1) * I],
                                 w[one].rearrange("o (c p) i -> p (o c) i", p=P)).then_inc(w_in, 16)
                sp.dma_start(w_dn[:, slot * WD_W:(slot + 1) * WD_W].rearrange("p (c n) -> p c n", c=2),
                             w_down[one].rearrange("o (c p) n -> p (o c) n", p=IH)).then_inc(w_in, 16)
                sp.wait_ge(w_in, (e + 1) * 48)
                sp.sem_inc(w_ready, 1)

            load_expert(0, 0)
            load_expert(1, 1)
            sp.wait_ge(lists_ready, 1)
            with sp.Fori(0, E // 2 - 1) as n:
                for slot in range(2):
                    last_tile = sp.value_load(lists[0:1, bass.ds(n * 2 + (LIST_END + slot), 1)],
                                              min_val=1, max_val=MAX_TILES)
                    sp.wait_ge(y_free, last_tile + 2)
                    load_expert(n * 2 + (2 + slot), slot)

            sp.wait_ge(moe_done, 1)
            for n in range(PIECES):
                for a in range(2):
                    src = acc_d[a][0:T, :].rearrange("(p r) d -> p (r d)", p=P)[:, n * PIECE:(n + 1) * PIECE]
                    sp.dma_start(addend(a, n), src).then_inc(sum_in[n], 16)
            for n in range(PIECES):
                sp.wait_ge(summed, n + 1)
                sp.dma_start(out.rearrange("b s d -> (b s) d").rearrange("(p r) d -> p (r d)", p=P)[:, n * PIECE:(n + 1) * PIECE],
                             addend(0, n)).then_inc(out_done, 16)
            sp.wait_ge(out_done, PIECES * 16)

        @block.gpsimd
        def _(pool):
            pool.memset(zeros[:, :], 0.0).then_inc(consts, 1)
            pool.iota(token_of[:, :], pattern=[[0, COLS + 1]], base=SPARE, channel_multiplier=1).then_inc(consts, 1)
            pool.memset(ident[:, :], 0.0).then_inc(consts, 1)
            pool.memset(earlier[:, :], 1.0).then_inc(consts, 1)
            pool.memset(ones[:, :], 1.0).then_inc(consts, 1)
            pool.memset(q_stage[:, :, :].bitcast(F32), 0.0).then_inc(consts, 1)
            pool.memset(k_stage[:, :, :].bitcast(F32), 0.0).then_inc(consts, 1)
            pool.memset(v_aug[0][:, :, :, :], 0.0).then_inc(consts, 1)
            pool.memset(v_aug[1][:, :, :, :], 0.0).then_inc(consts, 1)
            pool.iota(col_base[:, :, :], pattern=[[0, SC], [PLACES, E]], base=1, channel_multiplier=0,
                      allow_small_or_imprecise_dtypes=True).then_inc(consts, 1)
            pool.iota(tile_no[:, :], pattern=[[P, 2]], base=0, channel_multiplier=1,
                      allow_small_or_imprecise_dtypes=True).then_inc(consts, 1)
            pool.iota(expert_no[:, :], pattern=[[1, E]], base=0, channel_multiplier=0,
                      allow_small_or_imprecise_dtypes=True).then_inc(consts, 1)
            pool.iota(token[:, :], pattern=[[P, SC]], base=0, channel_multiplier=1,
                      allow_small_or_imprecise_dtypes=True).then_inc(consts, 1)
            pool.wait_ge(consts, 13)
            pool.affine_select(out=ident[:, :], in_=ident[:, :], compare_op=ALU.not_equal, fill=1.0, base=0,
                               pattern=[[-1, P]], channel_multiplier=1).then_inc(consts, 1)
            pool.affine_select(out=earlier[:, :], in_=earlier[:, :], compare_op=ALU.is_gt, fill=0.0, base=0,
                               pattern=[[1, P]], channel_multiplier=-1).then_inc(consts, 1)
            for c in range(SC):
                kk = k_stage[:, c, STK:].bitcast(F32).rearrange("p (k w) -> p k w", w=2 * STK)
                pool.memset(kk[:, :, 3 * DH:3 * DH + 2], -1.0).then_inc(consts, 1)
            for q in range(2):
                pool.memset(v_aug[q][:, :, :, DH:DH + 1], 1.0).then_inc(consts, 1)
            pool.wait_ge(consts, 19)

            def k_part(c, part):
                return k_stage[:, c, STK:].rearrange("p (k w) -> p k w", w=2 * STK)[:, :, part * DH:(part + 1) * DH]

            q_heads = q_stage[:, :, :].rearrange("p c (h w) -> p (c h) w", w=STK)
            xn_heads = xn[:, :, :].rearrange("p c (h w) -> p (c h) w", w=DH)
            STEPS = 8

            def stage(b, q, m, t_read):
                s0 = b * STEPS
                wait(pool, x_loaded[q], m * 32 + 32)
                wait(pool, t_free, t_read)
                wait(pool, o_free, (b - 1) * KV_HEADS if not isinstance(b, int) else max(0, (b - 1) * KV_HEADS))
                hold(pool, pool_step)
                pool.tensor_scalar(k_scaled[:, :, :], ctx_in[q][:, :, :], float(DH) ** -0.5, None,
                                   ALU.mult).then_inc(pool_step, 1)
                wait(pool, pool_step, s0 + 2)
                hold(pool, pool_step)
                for c in range(SC):
                    kc = k_scaled[:, c, :].rearrange("p (k w) -> p k w", w=DH)
                    pool.tensor_copy(v_aug[q][:, c, :, 0:DH], ctx_in[q][:, c, :].rearrange("p (k w) -> p k w", w=DH))
                    pool.tensor_copy(k_part(c, 0), kc)
                    i = pool.tensor_copy(k_part(c, 1), kc)
                i.then_inc(pool_step, 1)
                wait(pool, pool_step, s0 + 4)
                for c in range(SC):
                    kc = k_scaled[:, c, :].rearrange("p (k w) -> p k w", w=DH)
                    i = pool.tensor_tensor(k_part(c, 2), kc, k_part(c, 0).bitcast(F32), ALU.subtract)
                i.then_inc(pool_step, 1)
                wait(pool, xn_ready, (b + 1) * SC)
                hold(pool, pool_step)
                pool.tensor_copy(q_heads[:, :, 0:DH], xn_heads)
                pool.tensor_copy(q_heads[:, :, 2 * DH:3 * DH], xn_heads).then_inc(pool_step, 1)
                wait(pool, pool_step, s0 + 7)
                pool.tensor_tensor(q_heads[:, :, DH:2 * DH], xn_heads, q_heads[:, :, 0:DH].bitcast(F32),
                                   ALU.subtract).then_inc(pool_step, 1)
                wait(pool, pool_step, s0 + STEPS)
                pool.sem_inc(staged, 1)

            def scatter(b, q):
                wait(pool, token_sent, b * (SC * TOP_K * 16) + 16)
                pool.sem_inc(place_free, 1)
                wait(pool, place_ready, b + 1)
                hold(pool, pool_hold)
                for c in range(SC):
                    for n in range(TOP_K):
                        at = c * TOP_K + n
                        pool.indirect_dma_start(places_d, bass.IndirectOffsetOnAxis(place[q][:, at:at + 1].bitcast(U32), 0),
                                                token_i[q][:, c:c + 1], None).then_inc(token_sent, 16)

            pool_hold = idx_ready
            pool.sem_inc(place_free, 1)
            stage(0, 0, 0, 0)
            stage(1, 1, 0, T_START + 2 * KV_HEADS)
            pool.wait_ge(scratch_in, 16 * (1 + T // P - 4))

            def body(r):
                b, q = r.b, r.q
                if not (isinstance(b, int) and b < 2):
                    scatter(b - 2, q)
                if not (isinstance(b, int) and b + 2 >= B):
                    stage(b + 2, q, r.m + 1, r.t("K", KV_HEADS - 1) + 1)

            pool.dma_start(rows_d[SPARE:ROWS, :], zeros[:, :]).then_inc(token_sent, 16)
            for a in range(2):
                pool.dma_start(acc_d[a][SPARE:ROWS, :], zeros[:, 0:D]).then_inc(y_sent[a], 16)
            body(Round(0, 0))
            body(Round(1, 1))
            with pool.Fori(0, (B - 4) // 2) as n:
                body(Round(2 * n + 2, 0, n + 1))
                body(Round(2 * n + 3, 1, n + 1))
            for b in range(B - 2, B + 1):
                body(Round(b, b % 2))
            scatter(B - 1, (B - 1) % 2)
            HOLDS = B

            pool.wait_ge(token_sent, T // P * TOP_K * 16 + 16)
            pool.dma_start(token_of[:, 0:COLS], places_d.rearrange("(p c) o -> p (c o)", p=P)).then_inc(places_back, 16)
            pool.wait_ge(places_back, 16)
            for q in range(2):
                pool.wait_ge(rows_stored[q], 16 * B // 2 + 16)
                pool.wait_ge(x1_stored[q], 16 * B // 2 + 16)
            pool.wait_ge(lists_ready, 1)

            def column(i):
                at = slice(i, i + 1) if isinstance(i, int) else bass.ds(i, 1)
                col = pool.value_load(lists[0:1, at], min_val=0, max_val=COLS)
                return token_of[:, bass.ds(col, 1)]

            def gather(i, p, count):
                pool.tensor_copy(gather_idx[p][:, :], column(i)).then_inc(idx_ready, 1)
                pool.wait_ge(idx_ready, count + 1)
                hold(pool, idx_ready)
                pool.indirect_dma_start(xg[p], None, rows_d,
                                        bass.IndirectOffsetOnAxis(gather_idx[p][:, 0:1].bitcast(U32), 0)).then_inc(x_got[p], 16)

            def add_rows(i, p, n, count):
                pool.wait_ge(y_sent[p], n * 16 + 16)
                hold(pool, idx_ready)
                pool.tensor_copy(add_idx[p][:, :], column(i)).then_inc(idx_ready, 1)
                pool.wait_ge(idx_ready, count + 2)
                pool.wait_ge(y_free, i + 3)
                hold(pool, idx_ready)
                pool.indirect_dma_start(acc_d[p], bass.IndirectOffsetOnAxis(add_idx[p][:, 0:1].bitcast(U32), 0),
                                        y[p][:, :], None, compute_op=ALU.add).then_inc(y_sent[p], 16)

            gather(0, 0, HOLDS)
            gather(1, 1, HOLDS + 2)
            for i in range(2):
                pool.wait_ge(xt_full, i + 1)
                pool.wait_ge(wtok_ready, i + 1)
                gather(i + 2, i, HOLDS + 4 + 2 * i)
            pairs = pool.value_load(lists[0:1, LIST_PAIRS:LIST_PAIRS + 1], min_val=1, max_val=MAX_TILES // 2)
            with pool.Fori(0, pairs) as n:
                for p in range(2):
                    i = n * 2 + p
                    count = n * 12 + (HOLDS + 8 + 6 * p)
                    pool.wait_ge(xt_full, i + 3)
                    pool.wait_ge(wtok_ready, i + 3)
                    hold(pool, idx_ready)
                    gather(i + 4, p, count + 1)
                    add_rows(i, p, n, count + 3 - 0)
            for p in range(2):
                pool.wait_ge(y_sent[p], pairs * 16 + 16)
                pool.wait_ge(x_got[p], pairs * 16 + 32)
            pool.sem_inc(moe_done, 1)

        @block.tensor
        def _(pe):
            pe.wait_ge(consts, 19)
            pe.wait_ge(consts_in, 48)
            pe.wait_ge(gates_ready, 2)
            for c in range(DC):
                wait(pe, t_free, c)
                pe.transpose(t_ps[:, 0:E], router_sb[:, c * P:(c + 1) * P], ident[0:E, 0:E]).then_inc(t_full, 1)

            def transpose_q(t, j):
                wait(pe, t_free, t)
                for i in range(2):
                    for c in range(SC):
                        m = pe.transpose(t_psr[:, (i * SC + c) * P:(i * SC + c + 1) * P],
                                         q_stage[:, c, (2 * j + i) * P:(2 * j + i + 1) * P], ident_r[:, :])
                m.then_inc(t_full, 1)

            def transpose_k(t, j):
                wait(pe, t_free, t)
                for half in range(2):
                    for c in range(SC):
                        at = 2 * STK * j + (STK if half == 0 else 0)
                        m = pe.transpose(t_psr[:, (half * SC + c) * P:(half * SC + c + 1) * P],
                                         k_stage[:, c, at:at + P], ident_r[:, :])
                m.then_inc(t_full, 1)

            def scores_for_max(b, q, j, t_k):
                wait(pe, t_free, t_k + 1)
                for c in range(SC):
                    for i in range(2):
                        u = 2 * c + i
                        wait(pe, smax_free, b * (4 * KV_HEADS) + (4 * j + u - 1))
                        for half in range(2):
                            m = pe.matmul(s_max[u % 2][:, half * S:(half + 1) * S],
                                          qT[q][:, 2 * j + i, c * P:(c + 1) * P], kT[q][:, j, half, :],
                                          start=True, stop=True)
                        m.then_inc(smax_full, 1)

            def transpose_max(b, t):
                wait(pe, t_free, t)
                wait(pe, max_ready, b + 1)
                hold(pe, pe_hold)
                for c in range(SC):
                    m = pe.transpose(t_psr[0:2 * HEADS, c * P:(c + 1) * P], max_parts[:, c, :], ident_r[:, :])
                m.then_inc(t_full, 1)

            def scores_for_exp(b, q, j):
                for c in range(SC):
                    wait(pe, sexp_free, b * (2 * KV_HEADS) + (2 * j + c + 1))
                    for half in range(2):
                        m = pe.matmul(s_exp[c][:, half * 2 * S:(half + 1) * 2 * S],
                                      kT[q][:, j, half, c * P:(c + 1) * P], qT[q][:, 2 * j:2 * j + 2, :],
                                      start=True, stop=True)
                    m.then_inc(sexp_full, 1)

            def values(b, q, j):
                wait(pe, o_free, b * KV_HEADS + j)
                for c in range(SC):
                    wait(pe, sexp_free, b * (2 * KV_HEADS) + (2 * j + c + 3))
                    for half in range(2):
                        for i in range(2):
                            g = 2 * i + half
                            at = (2 * half + i) * S
                            m = pe.matmul(o_ps[32 * g:32 * g + 32, 0:S], v_aug[q][:, c, j, :],
                                          probs[j % 2][:, c, at:at + S], start=(c == 0), stop=(c == SC - 1),
                                          tile_position=(0, 32 * g))
                m.then_inc(o_full, 1)

            def transpose_o(b, t, j):
                wait(pe, t_free, t)
                wait(pe, o_free, b * KV_HEADS + (j + 2))
                for c in range(SC):
                    for i in range(2):
                        m = pe.transpose(t_ps[:, (2 * c + i) * P:(2 * c + i + 1) * P],
                                         oT[i][:, c * P:(c + 1) * P], ident[:, :])
                m.then_inc(t_full, 1)

            def transpose_rows(b, q, t, c):
                wait(pe, rows_ready, (b + 1) * SC)
                wait(pe, t_free, t)
                for n in range(DC):
                    m = pe.transpose(t_ps[:, n * P:(n + 1) * P], rows_sb[q][:, c, n * P:(n + 1) * P], ident[:, :])
                m.then_inc(t_full, 1)

            def router_logits(t):
                wait(pe, t_free, t)
                for c in range(SC):
                    for n in range(DC):
                        m = pe.matmul(t_ps[:, c * E:(c + 1) * E], xnT[:, c, n * P:(n + 1) * P], router_T[:, n, :],
                                      start=(n == 0), stop=(n == DC - 1))
                m.then_inc(t_full, 1)

            def ranks(b, t):
                wait(pe, t_free, t)
                wait(pe, mask_ready, b + 1)
                pe.matmul(t_ps[:, 0:E], earlier[:, :], mask_bf[:, 0, :], start=True, stop=True)
                pe.matmul(t_ps[:, E:2 * E], earlier[:, :], mask_bf[:, 1, :], start=True, stop=False)
                pe.matmul(t_ps[:, E:2 * E], ones[:, :], mask_bf[:, 0, :], start=False, stop=True)
                pe.matmul(t_ps[:, 2 * E:3 * E], ones[:, :], mask_bf[:, 0, :], start=True, stop=False)
                pe.matmul(t_ps[:, 2 * E:3 * E], ones[:, :], mask_bf[:, 1, :], start=False, stop=True).then_inc(t_full, 1)

            pe.wait_ge(staged, 1)
            for j in range(KV_HEADS):
                transpose_q(T_START + 2 * j, j)
                transpose_k(T_START + 2 * j + 1, j)
                scores_for_max(0, 0, j, T_START + 2 * j + 1)
            transpose_max(0, T_START + 2 * KV_HEADS)

            def body(r):
                b, q = r.b, r.q
                if r.tail_only:
                    transpose_rows(b - 1, 1 - q, r.t("X", 0), 0)
                    transpose_rows(b - 1, 1 - q, r.t("X", 1), 1)
                    router_logits(r.t("L"))
                    ranks(b - 1, r.t("R"))
                    return
                wait(pe, max_rows, (b + 1) * 64)
                if not r.last:
                    wait(pe, staged, b + 2)
                for j in range(KV_HEADS):
                    scores_for_exp(b, q, j)
                    if not r.last:
                        transpose_q(r.t("Q", j), j)
                        transpose_k(r.t("K", j), j)
                        if j:
                            scores_for_max(b + 1, 1 - q, j - 1, r.t("K", j - 1))
                    if j:
                        values(b, q, j - 1)
                    if j and j % 2 == 0:
                        transpose_o(b, r.t("O", j - 2), j - 2)
                    if not r.first:
                        if j == 2:
                            transpose_rows(b - 1, 1 - q, r.t("X", 0), 0)
                        if j == 3:
                            transpose_rows(b - 1, 1 - q, r.t("X", 1), 1)
                        if j == 4:
                            router_logits(r.t("L"))
                        if j == 6:
                            ranks(b - 1, r.t("R"))
                if not r.last:
                    scores_for_max(b + 1, 1 - q, KV_HEADS - 1, r.t("K", KV_HEADS - 1))
                values(b, q, KV_HEADS - 1)
                transpose_o(b, r.t("O", KV_HEADS - 2), KV_HEADS - 2)
                if not r.last:
                    transpose_max(b + 1, r.t("M"))

            rounds(pe, body)

            t_b = T_PRE + N_FIRST + (B - 2) * N_MID + N_LAST + len(U_TAIL)
            pe.wait_ge(vals_ready, 1)
            pe.wait_ge(t_free, t_b)
            for n in range(2):
                for c in range(2):
                    m = pe.matmul(t_ps[0:1, (2 * n + c) * P:(2 * n + c + 1) * P], tile_vals[:, c, n:n + 1],
                                  ident[:, :], start=True, stop=True)
            m.then_inc(lists_ps, 1)
            pe.wait_ge(lists_ready, 1)

            def transpose_x(i, p, n):
                pe.wait_ge(x_got[p], n * 16 + 16)
                for c in range(DC):
                    m = pe.transpose(xT_ps[:, c * P:(c + 1) * P], xg[p][:, c * P:(c + 1) * P], ident[:, :])
                m.then_inc(xt_full, 1)

            def expert_of(i):
                at = slice(LIST_E + i, LIST_E + i + 1) if isinstance(i, int) else bass.ds(i + LIST_E, 1)
                return pe.value_load(lists[0:1, at], min_val=0, max_val=E - 1)

            def gate_up(i, p):
                e = expert_of(i)
                off = pe.snap((e & 1) * GU_W)
                pe.wait_ge(w_ready, e + 1)
                pe.wait_ge(xt_ready, i + 1)
                for c in range(DC):
                    m = pe.matmul(gu_ps[p][:, 0:2 * I], xT[:, c * P:(c + 1) * P],
                                  w_gu[:, bass.ds(off + c * 2 * I, 2 * I)], start=(c == 0), stop=(c == DC - 1))
                m.then_inc(gu_full, 1)

            def transpose_h(i, p):
                pe.wait_ge(h_ready, i + 1)
                for c in range(2):
                    m = pe.transpose(hT_ps[0:IH, c * P:(c + 1) * P], h[p][:, c * IH:(c + 1) * IH], ident[:, :])
                m.then_inc(ht_full, 1)

            def down(i, p):
                off = pe.snap((expert_of(i) & 1) * WD_W)
                pe.wait_ge(ht_ready, i + 1)
                pe.wait_ge(y_free, i + 1)
                for c in range(2):
                    m = pe.matmul(y_ps[p], hT[:, c * P:(c + 1) * P], w_dn[:, bass.ds(off + c * D, D)],
                                  start=(c == 0), stop=(c == 1))
                m.then_inc(y_full, 1)

            transpose_x(0, 0, 0)
            pe.wait_ge(xt_ready, 1)
            transpose_x(1, 1, 0)
            gate_up(0, 0)
            pairs = pe.value_load(lists[0:1, LIST_PAIRS:LIST_PAIRS + 1], min_val=1, max_val=MAX_TILES // 2)
            with pe.Fori(0, pairs) as n:
                for p in range(2):
                    i = n * 2 + p
                    gate_up(i + 1, 1 - p)
                    transpose_h(i, p)
                    transpose_x(i + 2, p, n + 1)
                    down(i, p)

        @block.scalar
        def _(act):
            act.wait_ge(consts_in, 48)
            act.activation(gates[:, :], gates_in[:, :], ACT.Tanh).then_inc(gates_ready, 1)
            act.sem_inc(sexp_free, 2)

            def evac_q(t, q, j):
                wait(act, t_full, t + 1)
                act.copy(qT[q][:, 2 * j:2 * j + 2, :].rearrange("p a s -> p (a s)"), t_ps[:, :]).then_inc(t_free, 1)

            def exps(b, j):
                wait(act, o_full, b * KV_HEADS + (j - 1))
                for c in range(SC):
                    wait(act, sexp_full, b * (2 * KV_HEADS) + (2 * j + c + 1))
                    act.activation(probs[j % 2][:, c, :], s_exp[c][:, :], ACT.Exp).then_inc(sexp_free, 1)

            def evac_o(b, j):
                wait(act, o_full, b * KV_HEADS + (j + 1))
                act.copy(oT[j % 2][:, :], o_ps[:, 0:S]).then_inc(o_free, 1)

            def evac_rows(t, c):
                wait(act, t_full, t + 1)
                act.copy(xnT[:, c, :], t_ps[:, :]).then_inc(t_free, 1)

            def router_exp(b):
                wait(act, shifted, b + 1)
                act.activation(expd[:, :, :], logits[:, :, :], ACT.Exp).then_inc(expd_ready, 1)

            for j in range(KV_HEADS):
                evac_q(T_START + 2 * j, 0, j)

            def body(r):
                b, q = r.b, r.q
                if r.tail_only:
                    evac_rows(r.t("X", 0), 0)
                    evac_rows(r.t("X", 1), 1)
                    router_exp(b - 1)
                    return
                for j in range(KV_HEADS):
                    exps(b, j)
                    if not r.last:
                        evac_q(r.t("Q", j), 1 - q, j)
                    if j:
                        evac_o(b, j - 1)
                    if not r.first:
                        if j == 2:
                            evac_rows(r.t("X", 0), 0)
                        if j == 3:
                            evac_rows(r.t("X", 1), 1)
                        if j == 4:
                            router_exp(b - 1)
                evac_o(b, KV_HEADS - 1)

            rounds(act, body)

            act.wait_ge(lists_ready, 1)
            act.sem_inc(y_free, 2)
            pairs = act.value_load(lists[0:1, LIST_PAIRS:LIST_PAIRS + 1], min_val=1, max_val=MAX_TILES // 2)
            with act.Fori(0, pairs) as n:
                for p in range(2):
                    i = n * 2 + p
                    act.wait_ge(gu_full, i + 1)
                    act.activation(silu_g[p][:, :], gu_ps[p][:, 0:I], ACT.Silu).then_inc(silu_ready, 1)
                    act.wait_ge(y_sent[p], n * 16 + 16)
                    act.wait_ge(y_full, i + 1)
                    act.copy(y[p][:, :], y_ps[p]).then_inc(y_free, 1)

        @block.vector
        def _(dve):
            steps = [0]
            base = [0]

            def step(ins):
                ins.then_inc(dve_step, 1)
                steps[0] += 1

            def settle(held=False):
                wait(dve, dve_step, base[0] + steps[0])
                if held:
                    hold(dve, dve_step)
                    steps[0] += 1

            def broadcast(ap, n):
                return ap.unsqueeze(2).to_broadcast([ap.shape[0], ap.shape[1], n])

            dve.wait_ge(consts, 19)
            dve.tensor_copy(ident_r[:, :], ident[:, :]).then_inc(gates_ready, 1)
            dve.memset(counts[:, :], 0.0)
            dve.wait_ge(gates_ready, 2)
            for c in range(DC):
                wait(dve, t_full, c + 1)
                dve.tensor_copy(router_T[:, c, :], t_ps[:, 0:E]).then_inc(t_free, 1)

            def normalise(src, dst, ready):
                for c in range(SC):
                    step(dve.bn_stats(stats[:, c, :], src[:, c, :]))
                settle(True)
                for c in range(SC):
                    step(dve.bn_aggr(mean_var[:, c, :], stats[:, c, :]))
                settle()
                step(dve.tensor_scalar(var_eps[:, :], mean_var[:, :, 1], EPS, None, ALU.add))
                settle()
                step(dve.tensor_scalar(half_bits[:, :], var_eps[:, :].bitcast(I32), 1, None, ALU.logical_shift_right))
                step(dve.tensor_scalar(var_half[:, :], var_eps[:, :], -0.5, None, ALU.mult))
                settle()
                step(dve.tensor_scalar(rstd[:, :].bitcast(I32), half_bits[:, :], -1.0, ROOT_BITS, ALU.mult, ALU.add))
                settle()
                for _ in range(NEWTON):
                    step(dve.tensor_tensor(root_sq[:, :], rstd[:, :], rstd[:, :], ALU.mult))
                    settle()
                    step(dve.tensor_tensor(root_sq[:, :], root_sq[:, :], var_half[:, :], ALU.mult))
                    settle()
                    step(dve.scalar_tensor_tensor(out=rstd[:, :], in0=root_sq[:, :], scalar=1.5, in1=rstd[:, :],
                                                  op0=ALU.add, op1=ALU.mult))
                    settle()
                for c in range(SC):
                    dve.tensor_scalar(dst[:, c, 0:D], src[:, c, :], mean_var[:, c, 0:1], rstd[:, c:c + 1],
                                      ALU.subtract, ALU.mult).then_inc(ready, 1)

            def norm_x(b, q, m):
                wait(dve, x_loaded[q], m * 32 + 32)
                wait(dve, staged, b)
                normalise(x_in[q], xn, xn_ready)

            def evac_k(t, q, j):
                wait(dve, t_full, t + 1)
                dve.tensor_copy(kT[q][:, j, :, :].rearrange("p a s -> p (a s)"), t_ps[:, :]).then_inc(t_free, 1)

            def take_max(b, j):
                for c in range(SC):
                    for i in range(2):
                        u = 2 * c + i
                        wait(dve, smax_full, b * (4 * KV_HEADS) + (4 * j + u + 1))
                        dve.tensor_reduce(maxima[:, c, 4 * j + 2 * i:4 * j + 2 * i + 2],
                                          s_max[u % 2][:, :].rearrange("p (a s) -> p a s", a=2), AX.X,
                                          ALU.max).then_inc(smax_free, 1)

            def split_max(b):
                wait(dve, smax_free, (b + 1) * (4 * KV_HEADS))
                step(dve.tensor_copy(max_parts[:, :, 0:HEADS], maxima[:, :, :]))
                settle()
                dve.tensor_tensor(max_parts[:, :, HEADS:], maxima[:, :, :], max_parts[:, :, 0:HEADS].bitcast(F32),
                                  ALU.subtract).then_inc(max_ready, 1)

            def evac_max(b, t):
                wait(dve, t_full, t + 1)
                wait(dve, max_rows, b * 64)
                dve.tensor_copy(maxT[:, :], t_ps[0:2 * HEADS, 0:S]).then_inc(t_free, 1)

            def divide(t, j):
                wait(dve, t_full, t + 1)
                o = t_ps[:, :].rearrange("p (n w) -> p n w", w=32)
                step(dve.reciprocal(recip[:, :].unsqueeze(2), o[:, :, DH:DH + 1]))
                settle()
                rc = recip[:, :].rearrange("p (c n) -> p c n", c=SC).unsqueeze(3).to_broadcast([P, SC, 2 * G, DH])
                dst = attn[:, :, j * G * DH:(j + 2) * G * DH].rearrange("p c (n d) -> p c n d", d=DH)
                dve.tensor_tensor(dst, o[:, :, 0:DH].rearrange("p (c n) d -> p c n d", c=SC), rc,
                                  ALU.mult).then_inc(t_free, 1)
                steps.append(0)

            def residual(b, q, m):
                wait(dve, res_loaded[q], m * 16 + 16)
                wait(dve, x1_stored[q], m * 16 + 16)
                wait(dve, t_free, last_divide[0])
                dve.scalar_tensor_tensor(out=x1[q][:, :, :], in0=attn[:, :, :], scalar=gates[:, 0:1],
                                         in1=x_res[q][:, :, :], op0=ALU.mult, op1=ALU.add).then_inc(x1_ready, 1)
                wait(dve, x1_ready, b + 1)
                wait(dve, rows_stored[q], m * 16 + 16)
                normalise(x1[q], rows_sb[q], rows_ready)

            def route(b, q, t):
                wait(dve, t_full, t + 1)
                lg = t_ps[:, 0:SC * E].rearrange("p (c e) -> p c e", c=SC)
                step(dve.tensor_reduce(row2[:, 0, :], lg, AX.X, ALU.max))
                settle()
                dve.tensor_tensor(logits[:, :, :], lg, broadcast(row2[:, 0, :], E), ALU.subtract).then_inc(t_free, 1)
                wait(dve, t_free, t + 1)
                dve.sem_inc(shifted, 1)
                wait(dve, expd_ready, b + 1)
                step(dve.tensor_reduce(row2[:, 1, :], expd[:, :, :], AX.X, ALU.add))
                settle()
                step(dve.reciprocal(row2[:, 3, :], row2[:, 1, :]))
                settle()
                step(dve.tensor_tensor(pr[:, :, :], expd[:, :, :], broadcast(row2[:, 3, :], E), ALU.mult))
                settle(True)
                for c in range(SC):
                    step(dve.max(top[:, c, :], pr[:, c, :]))
                settle(True)
                for c in range(SC):
                    step(dve.match_replace(out=zapped[:, c, :], in_to_replace=top[:, c, :], in_values=pr[:, c, :],
                                           imm_value=-1.0))
                step(dve.tensor_reduce(row2[:, 2, :], top[:, :, :], AX.X, ALU.add))
                settle()
                step(dve.tensor_scalar(mask[:, :, :], zapped[:, :, :], 0.0, None, ALU.is_lt))
                dve.tensor_scalar(mask_bf[:, :, :], zapped[:, :, :], 0.0, None, ALU.is_lt).then_inc(mask_ready, 1)
                settle()
                step(dve.scalar_tensor_tensor(out=weighted[:, :, :], in0=pr[:, :, :], scalar=gates[:, 1:2],
                                              in1=mask[:, :, :], op0=ALU.mult, op1=ALU.mult))
                step(dve.reciprocal(row2[:, 0, :], row2[:, 2, :]))
                settle()
                dve.tensor_tensor(rows_sb[q][:, :, D:], weighted[:, :, :], broadcast(row2[:, 0, :], E),
                                  ALU.mult).then_inc(w_rows, 1)

            def find_places(b, q, t):
                wait(dve, t_full, t + 1)
                cb = counts[:, :].unsqueeze(1).to_broadcast([P, SC, E])
                step(dve.tensor_tensor(rank[:, :, :], t_ps[:, 0:SC * E].rearrange("p (c e) -> p c e", c=SC), cb, ALU.add))
                settle()
                dve.tensor_tensor(counts[:, :], counts[:, :], t_ps[:, SC * E:(SC + 1) * E], ALU.add).then_inc(t_free, 1)
                settle()
                step(dve.tensor_copy(rank_i[:, :, :], rank[:, :, :]))
                settle()
                step(dve.tensor_scalar(in_tile[:, :, :], rank_i[:, :, :], P - 1, COL_BITS, ALU.bitwise_and,
                                       ALU.logical_shift_left))
                step(dve.tensor_scalar(rank_i[:, :, :], rank_i[:, :, :], P_BITS, None, ALU.logical_shift_right))
                settle()
                step(dve.tensor_tensor(key[:, :, :], in_tile[:, :, :], rank_i[:, :, :], ALU.add))
                settle()
                step(dve.tensor_tensor(key[:, :, :], key[:, :, :], col_base[:, :, :], ALU.add))
                settle()
                step(dve.tensor_tensor(key[:, :, :], key[:, :, :], mask[:, :, :], ALU.mult))
                settle(True)
                for c in range(SC):
                    step(dve.max(top[:, c, :], key[:, c, :]))
                settle()
                wait(dve, place_free, b + 1)
                dve.tensor_scalar(place[q][:, :], top[:, :, :].rearrange("p c k -> p (c k)"), -1.0, None, ALU.add)
                step(dve.tensor_copy(token_i[q][:, :], token[:, :]))
                settle()
                dve.tensor_scalar(token[:, :], token[:, :], float(S), None, ALU.add).then_inc(place_ready, 1)

            last_divide = [0]
            norm_x(0, 0, 0)
            for j in range(KV_HEADS):
                evac_k(T_START + 2 * j + 1, 0, j)
                take_max(0, j)
            split_max(0)
            evac_max(0, T_START + 2 * KV_HEADS)
            norm_x(1, 1, 0)

            def body(r):
                b, q = r.b, r.q
                if not r.first:
                    u = U_FIRST if isinstance(b, int) and b == 1 else U_MID
                    if r.tail_only:
                        last_divide[0] = r.t0 - N_LAST + U_LAST[("O", KV_HEADS - 2)] + 1
                    else:
                        last_divide[0] = r.t0 - 1
                    residual(b - 1, 1 - q, (r.m if q == 1 else r.m - 1))
                if r.tail_only:
                    route(b - 1, 1 - q, r.t("L"))
                    find_places(b - 1, 1 - q, r.t("R"))
                    return
                for j in range(KV_HEADS):
                    if not r.last:
                        evac_k(r.t("K", j), 1 - q, j)
                        if j:
                            take_max(b + 1, j - 1)
                    if j and j % 2 == 0:
                        divide(r.t("O", j - 2), j - 2)
                    if not r.first:
                        if j == 4:
                            route(b - 1, 1 - q, r.t("L"))
                        if j == 6:
                            find_places(b - 1, 1 - q, r.t("R"))
                if not r.last:
                    take_max(b + 1, KV_HEADS - 1)
                divide(r.t("O", KV_HEADS - 2), KV_HEADS - 2)
                if not r.last:
                    split_max(b + 1)
                    evac_max(b + 1, r.t("M"))
                if not (r.last or (isinstance(b, int) and b + 2 >= B)):
                    norm_x(b + 2, q, r.m + 1)

            def stretch(r):
                steps[0] = 0
                body(r)
                return steps[0]

            base[0] = steps[0]
            base[0] += stretch(Round(0, 0))
            before = base[0]
            PER = DVE_STEPS
            with dve.Fori(0, (B - 4) // 2) as n:
                base[0] = n * (2 * PER) + before
                got = stretch(Round(2 * n + 1, 1, n))
                base[0] = n * (2 * PER) + (before + got)
                got2 = stretch(Round(2 * n + 2, 0, n + 1))
                assert got == got2 == PER, (got, got2)
            base[0] = before + (B - 4) * PER
            for b in range(B - 3, B + 1):
                base[0] += stretch(Round(b, b % 2))
            steps[0] = 0

            dve.wait_ge(place_ready, B)
            step(dve.tensor_scalar(n_tiles[:, :], counts[:, :], P - 1.0, None, ALU.add))
            settle()
            step(dve.tensor_copy(whole[:, :], n_tiles[:, :]))
            settle()
            step(dve.tensor_scalar(whole[:, :], whole[:, :], P_BITS, None, ALU.logical_shift_right))
            settle()
            step(dve.tensor_scalar(n_tiles[:, :], whole[:, :], 1.0, None, ALU.max))
            settle()
            step(dve.memset(started[:, :], 1.0))
            settle()
            step(dve.tensor_tensor_scan(tile_end[:, :], started[:, :], n_tiles[:, :], 0.0, ALU.mult, ALU.add))
            settle()
            for c in range(2):
                step(dve.tensor_scalar(started[:, :], tile_end[:, :], tile_no[:, c:c + 1], None, ALU.is_le))
                settle()
                step(dve.tensor_reduce(tile_vals[:, c, 1:2], started[:, :], AX.X, ALU.add))
                step(dve.tensor_tensor(started[:, :], started[:, :], n_tiles[:, :], ALU.mult))
                settle()
                step(dve.tensor_reduce(tile_vals[:, c, 2:3], started[:, :], AX.X, ALU.add))
                settle()
                step(dve.tensor_tensor(tile_vals[:, c, 3:4], tile_no[:, c:c + 1], tile_vals[:, c, 2:3], ALU.subtract))
                settle()
                step(dve.scalar_tensor_tensor(out=tile_vals[:, c, 0:1], in0=tile_vals[:, c, 1:2], scalar=float(PLACES),
                                              in1=tile_vals[:, c, 3:4], op0=ALU.mult, op1=ALU.add))
                settle()
                step(dve.tensor_scalar(tile_vals[:, c, 0:1], tile_vals[:, c, 0:1], float(COLS), None, ALU.min))
                step(dve.tensor_scalar(tile_vals[:, c, 1:2], tile_vals[:, c, 1:2], E - 1.0, None, ALU.min))
                settle()
            dve.sem_inc(vals_ready, 1)
            step(dve.tensor_copy(lists[0:1, LIST_END:LIST_END + E], tile_end[0:1, :]))
            step(dve.tensor_scalar(whole[0:1, 0:1], tile_end[0:1, E - 1:E], 1.0, None, ALU.add))
            settle()
            step(dve.tensor_scalar(lists[0:1, LIST_PAIRS:LIST_PAIRS + 1], whole[0:1, 0:1], 1, None,
                                   ALU.logical_shift_right))
            dve.wait_ge(lists_ps, 1)
            step(dve.tensor_copy(lists[0:1, 0:512], t_ps[0:1, 0:512]))
            settle()
            dve.sem_inc(lists_ready, 1)

            def expert_of(i):
                at = slice(LIST_E + i, LIST_E + i + 1) if isinstance(i, int) else bass.ds(i + LIST_E, 1)
                return dve.value_load(lists[0:1, at], min_val=0, max_val=E - 1)

            def evac_x(i, p):
                e = expert_of(i)
                dve.wait_ge(xt_full, i + 1)
                wait(dve, gu_full, i)
                dve.tensor_copy(xT[:, :], xT_ps[:, :]).then_inc(xt_ready, 1)
                dve.tensor_copy(w_tok[p][:, :], xg[p][:, bass.ds(e + D, 1)]).then_inc(wtok_ready, 1)

            evac_x(0, 0)
            evac_x(1, 1)
            pairs = dve.value_load(lists[0:1, LIST_PAIRS:LIST_PAIRS + 1], min_val=1, max_val=MAX_TILES // 2)
            with dve.Fori(0, pairs) as n:
                for p in range(2):
                    i = n * 2 + p
                    dve.wait_ge(wtok_ready, i + 1)
                    dve.wait_ge(silu_ready, i + 1)
                    dve.scalar_tensor_tensor(out=h[p][:, :], in0=silu_g[p][:, :], scalar=w_tok[p][:, 0:1],
                                             in1=gu_ps[p][:, I:2 * I], op0=ALU.mult, op1=ALU.mult).then_inc(h_ready, 1)
                    dve.wait_ge(ht_full, i + 1)
                    dve.tensor_copy(hT[:, :], hT_ps[0:IH, 0:2 * P]).then_inc(ht_ready, 1)
                    evac_x(i + 2, p)

            for n in range(PIECES):
                dve.wait_ge(sum_in[n], 32)
                dve.tensor_tensor(addend(0, n), addend(0, n), addend(1, n), ALU.add).then_inc(summed, 1)


DVE_STEPS = 72

_INS = ["x", "ctx_512", "g_xattn", "g_ffn", "L0_ffn_router_w", "L0_ffn_w_gate", "L0_ffn_w_up", "L0_ffn_w_down"]
_OUT = ((8, 256, 512), "float32")


def kernel(**inputs):
    import numpy as np
    import concourse.bacc as bacc
    from concourse.bass_utils import run_bass_kernel_spmd

    nc = bacc.Bacc("TRN2", target_bir_lowering=False, num_devices=1)
    arrays, args = {}, []
    for name in _INS:
        a = np.ascontiguousarray(inputs[name])
        arrays[f"in_{name}"] = a
        args.append(nc.dram_tensor(f"in_{name}", a.shape, mybir.dt.from_np(a.dtype), kind="ExternalInput").ap())
    args.append(nc.dram_tensor("out_0", _OUT[0], mybir.dt.from_np(np.dtype(_OUT[1])), kind="ExternalOutput").ap())
    flamingo_block(nc, *args)
    r = run_bass_kernel_spmd(nc, [arrays], core_ids=[0])
    return r.results[0]["out_0"]
```

```python
from contextlib import ExitStack

import concourse.bass as bass
from concourse import mybir

F32 = mybir.dt.float32
F32R = mybir.dt.float32r
BF16 = mybir.dt.bfloat16
I32 = mybir.dt.int32
U32 = mybir.dt.uint32
ALU = mybir.AluOpType
ACT = mybir.ActivationFunctionType
AX = mybir.AxisListType

P = 128
HEADS, KV_HEADS = 32, 8
TOP_K = 8
EPS = 1e-5
ROOT_BITS = float(0x5F3759DF)
NEWTON = 3


def flamingo_block(nc, x, ctx, g_xattn, g_ffn, router_w, w_gate, w_up, w_down, out):
    B, S, D = x.shape
    E, _, I = w_gate.shape
    DH = D // HEADS
    G = HEADS // KV_HEADS
    SC = S // P
    DC = D // P
    T = B * S
    SPARE = T
    ROWS = T + P
    XW = D + E
    PLACES = T // P
    COLS = E * PLACES
    IH = I // 2
    GU_W, WD_W = DC * 2 * I, 2 * D
    STK = 4 * DH
    PAIRS = HEADS // 2
    GROUPS = KV_HEADS // 2
    GH = HEADS // GROUPS
    MIN_TILES = 2
    MAX_TILES = T * TOP_K // P + MIN_TILES * E
    P_BITS, COL_BITS = P.bit_length() - 1, COLS.bit_length() - 1
    assert D == 512 and SC == 2 and B == 8 and STK == 64 and G == 4 and E == 32

    with ExitStack() as stack:
        def sb(name, shape, dt=F32):
            return stack.enter_context(nc.sbuf_tensor(name, shape, dt))

        def psum(name, shape):
            return stack.enter_context(nc.psum_tensor(name, shape, F32))

        def sem(name):
            return stack.enter_context(nc.semaphore(name))

        def two(make, name, *args):
            return [make(f"{name}{i}", *args) for i in range(2)]

        rows_d = nc.dram_tensor("expert_rows", [ROWS, XW], F32, kind="Internal").ap()
        places_d = nc.dram_tensor("places", [P * COLS, 1], I32, kind="Internal").ap()
        acc_d = [nc.dram_tensor(f"acc{i}", [ROWS, D], F32, kind="Internal").ap() for i in range(2)]

        ident = sb("ident", [P, P])
        ident_r = sb("ident_r", [P, P], F32R)
        earlier = sb("earlier", [P, P], BF16)
        ones = sb("ones", [P, P], BF16)
        zeros = sb("zeros", [P, XW])
        col_base = sb("col_base", [P, SC, E])
        tile_no = sb("tile_no", [P, 2])
        expert_no = sb("expert_no", [P, E])
        gates = sb("gates", [P, 2])
        gates_in = sb("gates_in", [P, 2])
        router_sb = sb("router_sb", [E, D])
        router_T = sb("router_T", [P, DC, E])

        x_in_both = sb("x_in", [P, 2 * SC * D])
        x_in = [x_in_both[:, i * SC * D:(i + 1) * SC * D].rearrange("p (c d) -> p c d", c=SC) for i in range(2)]
        ctx_in = two(sb, "ctx_in", [P, SC, KV_HEADS * DH])
        x_res = two(sb, "x_res", [P, SC, D])
        stats = sb("stats", [P, 2 * SC, 6])
        mean_var = sb("mean_var", [P, 2 * SC, 2])
        rstd = sb("rstd", [P, 2 * SC])
        var_eps = sb("var_eps", [P, 2 * SC]); var_half = sb("var_half", [P, 2 * SC])
        root_sq = sb("root_sq", [P, 2 * SC])
        half_bits = sb("half_bits", [P, 2 * SC], I32)
        xn = sb("xn", [P, SC, D])
        q_stage = sb("q_stage", [P, SC, HEADS * STK], F32R)
        k_stage = sb("k_stage", [P, SC, STK + KV_HEADS * 2 * STK], F32R)
        v_aug = two(sb, "v_aug", [P, SC, KV_HEADS, 32])
        qT = two(sb, "qT", [P, PAIRS, S], F32R)
        kT = two(sb, "kT", [P, KV_HEADS, 2, S], F32R)
        maxima = sb("maxima", [P, SC, HEADS])
        max_parts = sb("max_parts", [P, SC, 2 * HEADS], F32R)
        maxT = sb("maxT", [2 * HEADS, S], F32R)
        probs = two(sb, "probs", [P, SC, G * S])
        oT = two(sb, "oT", [P, S])
        recip = sb("recip", [P, 4 * G])
        attn = sb("attn", [P, SC, D])
        x1 = two(sb, "x1", [P, SC, D])
        rows_sb = two(sb, "rows_sb", [P, SC, XW])
        xnT = sb("xnT", [P, SC, D])
        logits = sb("logits", [P, SC, E])
        expd = sb("expd", [P, SC, E])
        row2 = sb("row2", [P, 4, SC])
        pr = sb("pr", [P, SC, E])
        top = sb("top", [P, SC, TOP_K])
        zapped = sb("zapped", [P, SC, E])
        mask = sb("mask", [P, SC, E])
        mask_bf = sb("mask_bf", [P, SC, E], BF16)
        weighted = sb("weighted", [P, SC, E])
        counts = sb("counts", [P, E])
        rank = sb("rank", [P, SC, E])
        rank_i = sb("rank_i", [P, SC, E], I32)
        in_tile = sb("in_tile", [P, SC, E], I32)
        key = sb("key", [P, SC, E])
        place = two(sb, "place", [P, SC * TOP_K], I32)
        token = sb("token", [P, SC])
        token_i = two(sb, "token_i", [P, SC], I32)

        n_tiles = sb("n_tiles", [P, E])
        tile_end = sb("tile_end", [P, E])
        started = sb("started", [P, E])
        whole = sb("whole", [P, E], I32)
        tile_vals = sb("tile_vals", [P, 2, 4])
        LIST_E, LIST_START, LIST_PAIRS = 256, 512, 512 + E + 1
        lists = sb("lists", [1, LIST_PAIRS + 1], I32)
        assert MAX_TILES + 4 <= LIST_E
        token_of = sb("token_of", [P, COLS + 1], I32)
        gather_idx = two(sb, "gather_idx", [P, 1], I32)
        add_idx = two(sb, "add_idx", [P, 1], I32)
        xg = [x_in[i][:, :, :].rearrange("p c d -> p (c d)")[:, 0:XW] for i in range(2)]
        w_tok = sb("w_tok", [P, 2])
        silu_g = sb("silu_g", [P, 2 * I])
        h_both = sb("h", [P, 2 * I])
        y_both = sb("y", [P, 2 * D])
        h = [h_both[:, i * I:(i + 1) * I] for i in range(2)]
        y = [y_both[:, i * D:(i + 1) * D] for i in range(2)]
        xT_hi = sb("xT_hi", [P, D], F32R); xT_lo = sb("xT_lo", [P, D], F32R)
        hT_hi = sb("hT_hi", [IH, 2 * P], F32R); hT_lo = sb("hT_lo", [IH, 2 * P], F32R)
        w_gu = sb("w_gu", [P, 2 * GU_W])
        w_dn = sb("w_dn", [IH, 2 * WD_W])
        gu_hi, gu_lo = (t[:, :, :].rearrange("p a s -> p (a s)") for t in qT)
        dn_hi, dn_lo = (t[0:IH, :, :, :].rearrange("p a c s -> p (a c s)") for t in kT)

        s_max_both = psum("s_max", [P, 4 * S])
        s_max = [s_max_both[:, i * 2 * S:(i + 1) * 2 * S] for i in range(2)]
        s_exp_both = psum("s_exp", [P, 2 * G * S])
        s_exp = [s_exp_both[:, i * G * S:(i + 1) * G * S] for i in range(2)]
        o_ps = psum("o_ps", [P, 512])
        t_ps = psum("t_ps", [P, 512])
        t_psr = t_ps[:, :].bitcast(F32R)
        gu_ps, hT_ps, xT_ps = s_max, o_ps, t_ps
        y_ps = [s_exp[i][:, 0:D] for i in range(2)]

        PIECES = 8
        PIECE = T * D // P // PIECES

        def addend(a, n):
            if a == 0 and n < 3:
                return w_gu[:, n * PIECE:(n + 1) * PIECE]
            if a == 1 and n < 4:
                return probs[n // 2][:, n % 2, :]
            t = (x_in[0], x_in[1], attn, xn, xnT)[n - 3] if a == 0 else (x_res + x1)[n - 4]
            return t[:, :, :].rearrange("p c d -> p (c d)")

        consts = sem("consts"); consts_in = sem("consts_in"); scratch_in = sem("scratch_in")
        gates_ready = sem("gates_ready")
        x_loaded = two(sem, "x_loaded"); res_loaded = two(sem, "res_loaded")
        xn_ready = sem("xn_ready"); hi_ready = sem("hi_ready"); staged = sem("staged"); v_copied = sem("v_copied")
        pool_hold = sem("pool_hold")
        dve_step = sem("dve_step"); pe_hold = sem("pe_hold"); place_free = sem("place_free")
        t_full = sem("t_full"); t_free = sem("t_free")
        smax_full = sem("smax_full"); smax_free = sem("smax_free")
        sexp_full = sem("sexp_full"); sexp_free = sem("sexp_free")
        o_full = sem("o_full"); o_free = sem("o_free")
        max_ready = sem("max_ready"); max_rows = sem("max_rows")
        x1_ready = sem("x1_ready"); rows_ready = sem("rows_ready"); w_rows = sem("w_rows")
        x1_stored = two(sem, "x1_stored"); rows_stored = two(sem, "rows_stored")
        shifted = sem("shifted"); expd_ready = sem("expd_ready"); mask_ready = sem("mask_ready")
        place_ready = sem("place_ready"); token_sent = sem("token_sent")
        vals_ready = sem("vals_ready"); lists_ps = sem("lists_ps"); lists_ready = sem("lists_ready")
        places_back = sem("places_back")
        w_in = sem("w_in"); w_ready = sem("w_ready")
        gu_hi_ready = sem("gu_hi_ready"); dn_hi_ready = sem("dn_hi_ready")
        gu_split = sem("gu_split"); dn_split = sem("dn_split")
        xhi_ready = sem("xhi_ready"); hthi_ready = sem("hthi_ready"); y_open = sem("y_open")
        x_got = two(sem, "x_got"); y_sent = two(sem, "y_sent")
        xt_full = sem("xt_full"); xt_ready = sem("xt_ready"); wtok_ready = sem("wtok_ready")
        gu_full = sem("gu_full"); silu_ready = sem("silu_ready"); h_ready = sem("h_ready")
        ht_full = sem("ht_full"); ht_ready = sem("ht_ready")
        y_full = sem("y_full"); y_free = sem("y_free"); idx_ready = sem("idx_ready")
        moe_done = sem("moe_done")
        sum_in = [sem(f"sum_in{i}") for i in range(PIECES)]; summed = sem("summed"); out_done = sem("out_done")

        def wait(eng, s, value):
            if not isinstance(value, int) or value > 0:
                eng.wait_ge(s, value)

        def hold(eng, s):
            eng.sem_inc(s, 1)

        def uses_of_round(first, last, tail_only=False):
            order = []
            if not tail_only:
                for j in range(KV_HEADS):
                    if not last:
                        order += [("Q", j), ("K", j)]
                    if j >= 3 and j % 2:
                        order.append(("O", j - 3))
                    if not first:
                        order += {2: [("X", 0)], 3: [("X", 1)], 4: [("L", 0)], 7: [("R", 0)]}.get(j, [])
                if not last:
                    order.append(("M", 0))
                order.append(("O", KV_HEADS - 2))
            else:
                order = [("X", 0), ("X", 1), ("L", 0), ("R", 0)]
            return {u: n for n, u in enumerate(order)}

        T_START = DC
        T_PRE = T_START + 2 * KV_HEADS + 1
        U_FIRST = uses_of_round(True, False)
        U_MID = uses_of_round(False, False)
        U_LAST = uses_of_round(False, True)
        U_TAIL = uses_of_round(False, False, True)
        N_FIRST, N_MID, N_LAST = len(U_FIRST), len(U_MID), len(U_LAST)

        class Round:

            def __init__(self, b, q, m=None):
                self.b, self.q = b, q
                self.m = m if m is not None else b // 2
                self.first = isinstance(b, int) and b == 0
                self.last = isinstance(b, int) and b == B - 1
                self.tail_only = isinstance(b, int) and b == B
                self.uses = U_FIRST if self.first else U_LAST if self.last else U_TAIL if self.tail_only else U_MID
                if self.first:
                    self.t0 = T_PRE
                elif self.tail_only:
                    self.t0 = T_PRE + N_FIRST + (B - 2) * N_MID + N_LAST
                else:
                    self.t0 = (b - 1) * N_MID + (T_PRE + N_FIRST)

            def t(self, kind, j=0):
                return self.t0 + self.uses[(kind, j)]

        def rounds(eng, body):
            body(Round(0, 0))
            with eng.Fori(0, (B - 4) // 2) as n:
                body(Round(2 * n + 1, 1, n))
                body(Round(2 * n + 2, 0, n + 1))
            for b in range(B - 3, B + 1):
                body(Round(b, b % 2))

        batch_rows = "(c p) d -> p c d"
        SCORE_SCALE = float(DH) ** -0.5

        def tiles_of_experts(eng, tile):
            def bound(e):
                at = slice(LIST_START + e, LIST_START + e + 1) if isinstance(e, int) else bass.ds(e + LIST_START, 1)
                return eng.value_load(lists[0:1, at], min_val=0, max_val=MAX_TILES)

            def expert(e, next_expert):
                first = bound(e)
                tile(first, next_expert)
                with eng.Fori(first + 1, bound(e + 1)) as i:
                    tile(i)

            with eng.Fori(0, E - 1) as e:
                expert(e, e + 1)
            expert(E - 1, None)

        def of_slot(t, e, width):
            return t[:, bass.ds((e & 1) * width, width)]

        def q_part(g, part):
            stacks = q_stage[:, :, g * GH * STK:(g + 1) * GH * STK].rearrange("p c (h w) -> p c h w", w=STK)
            return stacks[:, :, :, part * DH:(part + 1) * DH]

        def k_part(g, part):
            stacks = k_stage[:, :, STK + g * 4 * STK:STK + (g + 1) * 4 * STK].rearrange("p c (k w) -> p c k w", w=2 * STK)
            return stacks[:, :, :, part * DH:(part + 1) * DH]

        def xn_heads(g):
            return xn[:, :, g * GH * DH:(g + 1) * GH * DH].rearrange("p c (h w) -> p c h w", w=DH)

        def ctx_heads(q, g):
            return ctx_in[q][:, :, g * 2 * DH:(g + 1) * 2 * DH].rearrange("p c (k w) -> p c k w", w=DH)

        block = stack.enter_context(nc.Block())

        @block.sync
        def _(sp):
            def cut(t, b, n):
                return t[bass.ds(b * S, n * S), :] if not isinstance(b, int) else t[b * S:(b + n) * S, :]

            xf = x.rearrange("b s d -> (b s) d")
            cf = ctx.rearrange("b s d -> (b s) d")

            def load_x(b, q):
                sp.dma_start(x_in[q][:, :, :], cut(xf, b, 1).rearrange(batch_rows, p=P)).then_inc(x_loaded[q], 16)
                sp.dma_start(ctx_in[q][:, :, :], cut(cf, b, 1).rearrange(batch_rows, p=P)).then_inc(x_loaded[q], 16)

            def load_res(b, q):
                sp.dma_start(x_res[q][:, :, :], cut(xf, b, 1).rearrange(batch_rows, p=P)).then_inc(res_loaded[q], 16)

            def insert_max(b, q):
                wait(sp, t_free, b)
                for half in range(2):
                    for part in range(2):
                        at = STK * half + 3 * DH + part
                        sp.dma_start(qT[q][at:at + 1, :, :].bitcast(F32),
                                     maxT[HEADS * part + half:HEADS * (part + 1):2, :].bitcast(F32)).then_inc(max_rows, 16)

            load_x(0, 0)
            sp.dma_start(router_sb[:, :], router_w).then_inc(consts_in, 16)
            sp.dma_start(gates_in[:, 0:1], g_xattn.partition_broadcast(P)).then_inc(consts_in, 16)
            sp.dma_start(gates_in[:, 1:2], g_ffn.partition_broadcast(P)).then_inc(consts_in, 16)
            load_x(1, 1)
            load_res(0, 0)
            sp.wait_ge(consts, 8)
            sp.dma_start(places_d.rearrange("(p c) o -> p (c o)", p=P), token_of[:, 0:COLS]).then_inc(scratch_in, 16)
            for n in range(T // P):
                filled = (x1_stored + rows_stored)[n] if n < 4 else scratch_in
                sp.dma_start(acc_d[1][n * P:(n + 1) * P, :], zeros[:, 0:D]).then_inc(filled, 16)
            def load_after(b, q):
                wait(sp, staged, (b - 1) * GROUPS)
                wait(sp, v_copied, b - 1)
                load_x(b, q)

            load_after(2, 0)
            insert_max(T_PRE, 0)

            def body(r):
                b, q = r.b, r.q
                if not r.first:
                    wait(sp, x1_ready, b)
                    sp.dma_start(cut(acc_d[0], b - 1, 1).rearrange(batch_rows, p=P),
                                 x1[1 - q][:, :, :]).then_inc(x1_stored[1 - q], 16)
                if not r.tail_only and not r.last:
                    load_res(b + 1, 1 - q)
                if not (isinstance(b, int) and b + 3 >= B):
                    load_after(b + 3, 1 - q)
                if not r.first:
                    wait(sp, w_rows, b)
                    sp.dma_start(cut(rows_d, b - 1, 1).rearrange(batch_rows, p=P),
                                 rows_sb[1 - q][:, :, :]).then_inc(rows_stored[1 - q], 16)
                if not r.tail_only and not r.last:
                    insert_max(r.t("M") + 1, 1 - q)

            rounds(sp, body)

            def load_expert(e, slot):
                one = (slice(e, e + 1) if isinstance(e, int) else bass.ds(e, 1))
                gu = w_gu[:, slot * GU_W:(slot + 1) * GU_W].rearrange("p (c n) -> p c n", c=DC)
                for n, w in enumerate((w_gate, w_up)):
                    sp.dma_start(gu[:, :, n * I:(n + 1) * I],
                                 w[one].rearrange("o (c p) i -> p (o c) i", p=P)).then_inc(w_in, 16)
                sp.dma_start(w_dn[:, slot * WD_W:(slot + 1) * WD_W].rearrange("p (c n) -> p c n", c=2),
                             w_down[one].rearrange("o (c p) n -> p (o c) n", p=IH)).then_inc(w_in, 16)
                sp.wait_ge(w_in, (e + 1) * 48)
                sp.sem_inc(w_ready, 1)

            load_expert(0, 0)
            load_expert(1, 1)
            with sp.Fori(1, E // 2) as n:
                for slot in range(2):
                    sp.wait_ge(gu_split, n * 2 + (slot - 1))
                    sp.wait_ge(dn_split, n * 2 + (slot - 1))
                    load_expert(n * 2 + slot, slot)

            sp.wait_ge(moe_done, 1)
            for n in range(PIECES):
                for a in range(2):
                    src = acc_d[a][0:T, :].rearrange("(p r) d -> p (r d)", p=P)[:, n * PIECE:(n + 1) * PIECE]
                    sp.dma_start(addend(a, n), src).then_inc(sum_in[n], 16)
            for n in range(PIECES):
                sp.wait_ge(summed, n + 1)
                sp.dma_start(out.rearrange("b s d -> (b s) d").rearrange("(p r) d -> p (r d)", p=P)[:, n * PIECE:(n + 1) * PIECE],
                             addend(0, n)).then_inc(out_done, 16)
            sp.wait_ge(out_done, PIECES * 16)

        @block.gpsimd
        def _(pool):
            pool.memset(zeros[:, :], 0.0).then_inc(consts, 1)
            pool.iota(token_of[:, :], pattern=[[0, COLS + 1]], base=SPARE, channel_multiplier=1).then_inc(consts, 1)
            pool.memset(ident[:, :], 0.0).then_inc(consts, 1)
            pool.memset(earlier[:, :], 1.0).then_inc(consts, 1)
            pool.memset(ones[:, :], 1.0).then_inc(consts, 1)
            pool.memset(q_stage[:, :, :].bitcast(F32), 0.0).then_inc(consts, 1)
            pool.memset(k_stage[:, :, :].bitcast(F32), 0.0).then_inc(consts, 1)
            pool.memset(v_aug[0][:, :, :, :], 0.0).then_inc(consts, 1)
            pool.memset(v_aug[1][:, :, :, :], 0.0).then_inc(consts, 1)
            pool.iota(col_base[:, :, :], pattern=[[0, SC], [PLACES, E]], base=1, channel_multiplier=0,
                      allow_small_or_imprecise_dtypes=True).then_inc(consts, 1)
            pool.iota(tile_no[:, :], pattern=[[P, 2]], base=0, channel_multiplier=1,
                      allow_small_or_imprecise_dtypes=True).then_inc(consts, 1)
            pool.iota(expert_no[:, :], pattern=[[1, E]], base=0, channel_multiplier=0,
                      allow_small_or_imprecise_dtypes=True).then_inc(consts, 1)
            pool.iota(token[:, :], pattern=[[P, SC]], base=0, channel_multiplier=1,
                      allow_small_or_imprecise_dtypes=True).then_inc(consts, 1)
            pool.wait_ge(consts, 13)
            pool.affine_select(out=ident[:, :], in_=ident[:, :], compare_op=ALU.not_equal, fill=1.0, base=0,
                               pattern=[[-1, P]], channel_multiplier=1).then_inc(consts, 1)
            pool.affine_select(out=earlier[:, :], in_=earlier[:, :], compare_op=ALU.is_gt, fill=0.0, base=0,
                               pattern=[[1, P]], channel_multiplier=-1).then_inc(consts, 1)
            for c in range(SC):
                kk = k_stage[:, c, STK:].bitcast(F32).rearrange("p (k w) -> p k w", w=2 * STK)
                pool.memset(kk[:, :, 3 * DH:3 * DH + 2], -1.0).then_inc(consts, 1)
            for q in range(2):
                pool.memset(v_aug[q][:, :, :, DH:DH + 1], 1.0).then_inc(consts, 1)
            pool.wait_ge(consts, 19)


            def stage_lo(b, q, m, g):
                wait(pool, hi_ready, b * GROUPS + (g + 1))
                pool.tensor_tensor(q_part(g, 1), xn_heads(g), q_part(g, 0).bitcast(F32), ALU.subtract)
                pool.tensor_tensor(k_part(g, 2), ctx_heads(q, g), k_part(g, 0).bitcast(F32),
                                   ALU.subtract).then_inc(staged, 1)

            def copy_v(b, q, m):
                wait(pool, x_loaded[q], m * 32 + 32)
                wait(pool, o_full, (b - 1) * KV_HEADS)
                hold(pool, pool_hold)
                for c in range(SC):
                    i = pool.tensor_copy(v_aug[q][:, c, :, 0:DH],
                                         ctx_in[q][:, c, :].rearrange("p (k w) -> p k w", w=DH))
                i.then_inc(v_copied, 1)

            def scatter(b, q, at_once):
                if at_once.start == 0:
                    wait(pool, token_sent, b * (SC * TOP_K * 16) + 16)
                    pool.sem_inc(place_free, 1)
                    wait(pool, place_ready, b + 1)
                    hold(pool, pool_hold)
                for at in at_once:
                    c = at // TOP_K
                    pool.indirect_dma_start(places_d, bass.IndirectOffsetOnAxis(place[q][:, at:at + 1].bitcast(U32), 0),
                                            token_i[q][:, c:c + 1], None).then_inc(token_sent, 16)

            pool.sem_inc(place_free, 1)
            for g in range(GROUPS):
                stage_lo(0, 0, 0, g)
            copy_v(0, 0, 0)
            for g in range(GROUPS):
                stage_lo(1, 1, 0, g)
            pool.wait_ge(scratch_in, 16 * (1 + T // P - 4))

            def body(r):
                b, q = r.b, r.q
                if not (r.last or r.tail_only):
                    copy_v(b + 1, 1 - q, (r.m if q == 0 else r.m + 1))
                per = SC * TOP_K // GROUPS
                for g in range(GROUPS):
                    if not (isinstance(b, int) and b < 2):
                        scatter(b - 2, q, range(g * per, (g + 1) * per))
                    if not (isinstance(b, int) and b + 2 >= B):
                        stage_lo(b + 2, q, r.m + 1, g)

            pool.dma_start(rows_d[SPARE:ROWS, :], zeros[:, :]).then_inc(token_sent, 16)
            for a in range(2):
                pool.dma_start(acc_d[a][SPARE:ROWS, :], zeros[:, 0:D]).then_inc(y_sent[a], 16)
            body(Round(0, 0))
            body(Round(1, 1))
            with pool.Fori(0, (B - 4) // 2) as n:
                body(Round(2 * n + 2, 0, n + 1))
                body(Round(2 * n + 3, 1, n + 1))
            for b in range(B - 2, B + 1):
                body(Round(b, b % 2))
            scatter(B - 1, (B - 1) % 2, range(SC * TOP_K))

            pool.wait_ge(token_sent, T // P * TOP_K * 16 + 16)
            pool.dma_start(token_of[:, 0:COLS], places_d.rearrange("(p c) o -> p (c o)", p=P)).then_inc(places_back, 16)
            pool.wait_ge(places_back, 16)
            for q in range(2):
                pool.wait_ge(rows_stored[q], 16 * B // 2 + 16)
                pool.wait_ge(x1_stored[q], 16 * B // 2 + 16)
            pool.wait_ge(lists_ready, 1)

            def column(i):
                at = slice(i, i + 1) if isinstance(i, int) else bass.ds(i, 1)
                col = pool.value_load(lists[0:1, at], min_val=0, max_val=COLS)
                return token_of[:, bass.ds(col, 1)]

            def gather(i, p, count):
                pool.tensor_copy(gather_idx[p][:, :], column(i)).then_inc(idx_ready, 1)
                pool.wait_ge(idx_ready, count + 1)
                hold(pool, idx_ready)
                pool.indirect_dma_start(xg[p], None, rows_d,
                                        bass.IndirectOffsetOnAxis(gather_idx[p][:, 0:1].bitcast(U32), 0)).then_inc(x_got[p], 16)

            def add_rows(i, p, n, count):
                pool.tensor_copy(add_idx[p][:, :], column(i)).then_inc(idx_ready, 1)
                pool.wait_ge(idx_ready, count + 1)
                pool.wait_ge(y_free, i + 3)
                hold(pool, idx_ready)
                pool.indirect_dma_start(acc_d[p], bass.IndirectOffsetOnAxis(add_idx[p][:, 0:1].bitcast(U32), 0),
                                        y[p][:, :], None, compute_op=ALU.add).then_inc(y_sent[p], 16)

            gather(0, 0, 0)
            gather(1, 1, 2)
            for i in range(2):
                pool.wait_ge(xt_full, i + 1)
                pool.wait_ge(wtok_ready, i + 1)
                gather(i + 2, i, 4 + 2 * i)
            pairs = pool.value_load(lists[0:1, LIST_PAIRS:LIST_PAIRS + 1], min_val=1, max_val=MAX_TILES // 2)
            with pool.Fori(0, pairs) as n:
                for p in range(2):
                    i = n * 2 + p
                    count = n * 10 + (8 + 5 * p)
                    pool.wait_ge(y_sent[p], n * 16 + 16)
                    pool.sem_inc(y_open, 1)
                    pool.wait_ge(xt_full, i + 3)
                    pool.wait_ge(wtok_ready, i + 3)
                    hold(pool, idx_ready)
                    gather(i + 4, p, count + 1)
                    add_rows(i, p, n, count + 3)
            for p in range(2):
                pool.wait_ge(y_sent[p], pairs * 16 + 16)
                pool.wait_ge(x_got[p], pairs * 16 + 32)
            pool.sem_inc(moe_done, 1)

        @block.tensor
        def _(pe):
            pe.wait_ge(consts, 19)
            pe.wait_ge(consts_in, 48)
            pe.wait_ge(gates_ready, 2)
            for c in range(DC):
                wait(pe, t_free, c)
                pe.transpose(t_ps[:, 0:E], router_sb[:, c * P:(c + 1) * P], ident[0:E, 0:E]).then_inc(t_full, 1)

            def transpose_q(t, j):
                wait(pe, t_free, t)
                for i in range(2):
                    for c in range(SC):
                        m = pe.transpose(t_psr[:, (i * SC + c) * P:(i * SC + c + 1) * P],
                                         q_stage[:, c, (2 * j + i) * P:(2 * j + i + 1) * P], ident_r[:, :])
                m.then_inc(t_full, 1)

            def transpose_k(t, j):
                wait(pe, t_free, t)
                for half in range(2):
                    for c in range(SC):
                        at = 2 * STK * j + (STK if half == 0 else 0)
                        m = pe.transpose(t_psr[:, (half * SC + c) * P:(half * SC + c + 1) * P],
                                         k_stage[:, c, at:at + P], ident_r[:, :])
                m.then_inc(t_full, 1)

            def scores_for_max(b, q, j, t_k, parts):
                wait(pe, t_free, t_k + 1)
                for u in parts:
                    c, i = u // 2, u % 2
                    wait(pe, smax_free, b * (4 * KV_HEADS) + (4 * j + u - 1))
                    for half in range(2):
                        m = pe.matmul(s_max[u % 2][:, half * S:(half + 1) * S],
                                      qT[q][:, 2 * j + i, c * P:(c + 1) * P], kT[q][:, j, half, :],
                                      start=True, stop=True)
                    m.then_inc(smax_full, 1)

            def transpose_max(b, t):
                wait(pe, t_free, t)
                wait(pe, max_ready, b + 1)
                hold(pe, pe_hold)
                for c in range(SC):
                    m = pe.transpose(t_psr[0:2 * HEADS, c * P:(c + 1) * P], max_parts[:, c, :], ident_r[:, :])
                m.then_inc(t_full, 1)

            def scores_for_exp(b, q, j, c):
                wait(pe, sexp_free, b * (2 * KV_HEADS) + (2 * j + c + 1))
                for half in range(2):
                    m = pe.matmul(s_exp[c][:, half * 2 * S:(half + 1) * 2 * S],
                                  kT[q][:, j, half, c * P:(c + 1) * P], qT[q][:, 2 * j:2 * j + 2, :],
                                  start=True, stop=True)
                m.then_inc(sexp_full, 1)

            def values(b, q, j):
                wait(pe, o_free, b * KV_HEADS + j)
                for c in range(SC):
                    wait(pe, sexp_free, b * (2 * KV_HEADS) + (2 * j + c + 3))
                    for half in range(2):
                        for i in range(2):
                            g = 2 * i + half
                            at = (2 * half + i) * S
                            m = pe.matmul(o_ps[32 * g:32 * g + 32, 0:S], v_aug[q][:, c, j, :],
                                          probs[j % 2][:, c, at:at + S], start=(c == 0), stop=(c == SC - 1),
                                          tile_position=(0, 32 * g))
                m.then_inc(o_full, 1)

            def transpose_o(b, t, j):
                wait(pe, t_free, t)
                wait(pe, o_free, b * KV_HEADS + (j + 2))
                for c in range(SC):
                    for i in range(2):
                        m = pe.transpose(t_ps[:, (2 * c + i) * P:(2 * c + i + 1) * P],
                                         oT[i][:, c * P:(c + 1) * P], ident[:, :])
                m.then_inc(t_full, 1)

            def transpose_rows(b, q, t, c):
                wait(pe, rows_ready, (b + 1) * SC)
                wait(pe, t_free, t)
                for n in range(DC):
                    m = pe.transpose(t_ps[:, n * P:(n + 1) * P], rows_sb[q][:, c, n * P:(n + 1) * P], ident[:, :])
                m.then_inc(t_full, 1)

            def router_logits(t):
                wait(pe, t_free, t)
                for c in range(SC):
                    for n in range(DC):
                        m = pe.matmul(t_ps[:, c * E:(c + 1) * E], xnT[:, c, n * P:(n + 1) * P], router_T[:, n, :],
                                      start=(n == 0), stop=(n == DC - 1))
                m.then_inc(t_full, 1)

            def ranks(b, t):
                wait(pe, t_free, t)
                wait(pe, mask_ready, b + 1)
                pe.matmul(t_ps[:, 0:E], earlier[:, :], mask_bf[:, 0, :], start=True, stop=True)
                pe.matmul(t_ps[:, E:2 * E], earlier[:, :], mask_bf[:, 1, :], start=True, stop=False)
                pe.matmul(t_ps[:, E:2 * E], ones[:, :], mask_bf[:, 0, :], start=False, stop=True)
                pe.matmul(t_ps[:, 2 * E:3 * E], ones[:, :], mask_bf[:, 0, :], start=True, stop=False)
                pe.matmul(t_ps[:, 2 * E:3 * E], ones[:, :], mask_bf[:, 1, :], start=False, stop=True).then_inc(t_full, 1)

            for j in range(KV_HEADS):
                pe.wait_ge(staged, j // 2 + 1)
                transpose_q(T_START + 2 * j, j)
                transpose_k(T_START + 2 * j + 1, j)
                scores_for_max(0, 0, j, T_START + 2 * j + 1, range(4))
            transpose_max(0, T_START + 2 * KV_HEADS)

            def body(r):
                b, q = r.b, r.q
                if r.tail_only:
                    transpose_rows(b - 1, 1 - q, r.t("X", 0), 0)
                    transpose_rows(b - 1, 1 - q, r.t("X", 1), 1)
                    router_logits(r.t("L"))
                    ranks(b - 1, r.t("R"))
                    return

                def next_max(j, parts):
                    if j >= 0 and not r.last:
                        scores_for_max(b + 1, 1 - q, j, r.t("K", j), parts)

                for j in range(KV_HEADS):
                    if not r.last:
                        wait(pe, staged, (b + 1) * GROUPS + (j // 2 + 1))
                        transpose_q(r.t("Q", j), j)
                    next_max(j - 1, (0, 1))
                    if j:
                        scores_for_exp(b, q, j, 0)
                    if not r.last:
                        transpose_k(r.t("K", j), j)
                    if j == 0:
                        wait(pe, max_rows, (b + 1) * 64)
                        scores_for_exp(b, q, j, 0)
                    next_max(j - 1, (2,))
                    scores_for_exp(b, q, j, 1)
                    next_max(j - 1, (3,))
                    if j >= 3 and j % 2:
                        transpose_o(b, r.t("O", j - 3), j - 3)
                    if j == 1:
                        wait(pe, v_copied, b + 1)
                    if j:
                        values(b, q, j - 1)
                    if not r.first:
                        if j == 2:
                            transpose_rows(b - 1, 1 - q, r.t("X", 0), 0)
                        if j == 3:
                            transpose_rows(b - 1, 1 - q, r.t("X", 1), 1)
                        if j == 4:
                            router_logits(r.t("L"))
                        if j == 7:
                            ranks(b - 1, r.t("R"))
                next_max(KV_HEADS - 1, range(4))
                values(b, q, KV_HEADS - 1)
                if not r.last:
                    transpose_max(b + 1, r.t("M"))
                transpose_o(b, r.t("O", KV_HEADS - 2), KV_HEADS - 2)

            rounds(pe, body)

            t_b = T_PRE + N_FIRST + (B - 2) * N_MID + N_LAST + len(U_TAIL)
            pe.wait_ge(vals_ready, 1)
            pe.wait_ge(t_free, t_b)
            for n in range(2):
                for c in range(2):
                    m = pe.matmul(t_ps[0:1, (2 * n + c) * P:(2 * n + c + 1) * P], tile_vals[:, c, n:n + 1],
                                  ident[:, :], start=True, stop=True)
            m.then_inc(lists_ps, 1)
            pe.wait_ge(lists_ready, 1)

            def transpose_x(i, p, n):
                pe.wait_ge(x_got[p], n * 16 + 16)
                for c in range(DC):
                    m = pe.transpose(xT_ps[:, c * P:(c + 1) * P], xg[p][:, c * P:(c + 1) * P], ident[:, :])
                m.then_inc(xt_full, 1)

            def expert_of(i):
                at = slice(LIST_E + i, LIST_E + i + 1) if isinstance(i, int) else bass.ds(i + LIST_E, 1)
                return pe.value_load(lists[0:1, at], min_val=0, max_val=E - 1)

            def transpose_h(i, p):
                pe.wait_ge(h_ready, i + 1)
                for c in range(2):
                    m = pe.transpose(hT_ps[0:IH, c * P:(c + 1) * P], h[p][:, c * IH:(c + 1) * IH], ident[:, :])
                m.then_inc(ht_full, 1)

            def gate_up(i, p, e, between=None):
                off = pe.snap((e & 1) * GU_W)
                pe.wait_ge(gu_split, e + 1)
                pe.wait_ge(xhi_ready, i + 1)
                for c in range(DC):
                    for w in (gu_hi, gu_lo):
                        pe.matmul(gu_ps[p][:, 0:2 * I], xT_hi[:, c * P:(c + 1) * P],
                                  w[:, c * 2 * I:c * 2 * I + GU_W + 2 * I][:, bass.ds(off, 2 * I)],
                                  start=(c == 0 and w is gu_hi), stop=False)
                if between:
                    between()
                pe.wait_ge(xt_ready, i + 1)
                for c in range(DC):
                    m = pe.matmul(gu_ps[p][:, 0:2 * I], xT_lo[:, c * P:(c + 1) * P],
                                  gu_hi[:, c * 2 * I:c * 2 * I + GU_W + 2 * I][:, bass.ds(off, 2 * I)],
                                  start=False, stop=(c == DC - 1))
                m.then_inc(gu_full, 1)

            def down(i, p, e):
                off = pe.snap((e & 1) * WD_W)
                pe.wait_ge(dn_split, e + 1)
                pe.wait_ge(hthi_ready, i + 1)
                pe.wait_ge(y_free, i + 1)
                for c in range(2):
                    for w in (dn_hi, dn_lo):
                        pe.matmul(y_ps[p], hT_hi[:, c * P:(c + 1) * P], w[:, c * D:c * D + WD_W + D][:, bass.ds(off, D)],
                                  start=(c == 0 and w is dn_hi), stop=False)
                pe.wait_ge(ht_ready, i + 1)
                for c in range(2):
                    m = pe.matmul(y_ps[p], hT_lo[:, c * P:(c + 1) * P], dn_hi[:, c * D:c * D + WD_W + D][:, bass.ds(off, D)],
                                  start=False, stop=(c == 1))
                m.then_inc(y_full, 1)

            transpose_x(0, 0, 0)
            pe.wait_ge(xt_ready, 1)
            transpose_x(1, 1, 0)
            gate_up(0, 0, 0)
            pairs = pe.value_load(lists[0:1, LIST_PAIRS:LIST_PAIRS + 1], min_val=1, max_val=MAX_TILES // 2)
            carried = [pe.alloc_register(f"expert_of_next{k}") for k in range(2)]
            for k in range(2):
                pe.reg_mov(carried[k], expert_of(k))
            with pe.Fori(0, pairs) as n:
                e = [pe.snap(reg, min_val=0, max_val=E - 1) for reg in carried]
                for p in range(2):
                    i = n * 2 + p
                    gate_up(i + 1, 1 - p, e[p + 1], lambda i=i, p=p: transpose_h(i, p))
                    transpose_x(i + 2, p, n + 1)
                    e.append(expert_of(i + 2))
                    down(i, p, e[p])
                for k in range(2):
                    pe.reg_mov(carried[k], e[k + 2])

        @block.scalar
        def _(act):
            act.wait_ge(consts_in, 48)
            act.activation(gates[:, :], gates_in[:, :], ACT.Tanh).then_inc(gates_ready, 1)
            act.sem_inc(sexp_free, 2)

            def stage_hi(b, q, m, g):
                wait(act, x_loaded[q], m * 32 + 32)
                wait(act, xn_ready, (b + 1) * SC)
                for part in (0, 2):
                    act.copy(q_part(g, part), xn_heads(g))
                for part in (0, 1):
                    i = act.copy(k_part(g, part), ctx_heads(q, g))
                i.then_inc(hi_ready, 1)

            def evac_q(t, q, j):
                wait(act, t_full, t + 1)
                act.copy(qT[q][:, 2 * j:2 * j + 2, :].rearrange("p a s -> p (a s)"), t_ps[:, :]).then_inc(t_free, 1)

            def evac_k(t, q, j):
                wait(act, t_full, t + 1)
                act.copy(kT[q][:, j, :, :].rearrange("p a s -> p (a s)"), t_ps[:, :]).then_inc(t_free, 1)

            def exps(b, j, c):
                wait(act, o_full, b * KV_HEADS + (j - 1))
                wait(act, sexp_full, b * (2 * KV_HEADS) + (2 * j + c + 1))
                act.activation(probs[j % 2][:, c, :], s_exp[c][:, :], ACT.Exp,
                               scale=SCORE_SCALE).then_inc(sexp_free, 1)

            def evac_o(b, j):
                wait(act, o_full, b * KV_HEADS + (j + 1))
                act.copy(oT[j % 2][:, :], o_ps[:, 0:S]).then_inc(o_free, 1)

            def evac_rows(t, c):
                wait(act, t_full, t + 1)
                act.copy(xnT[:, c, :], t_ps[:, :]).then_inc(t_free, 1)

            def router_exp(b):
                wait(act, shifted, b + 1)
                act.activation(expd[:, :, :], logits[:, :, :], ACT.Exp).then_inc(expd_ready, 1)

            act.wait_ge(consts, 19)
            for g in range(GROUPS):
                stage_hi(0, 0, 0, g)
            for j in range(KV_HEADS):
                evac_q(T_START + 2 * j, 0, j)
                evac_k(T_START + 2 * j + 1, 0, j)
                if j % 2:
                    stage_hi(1, 1, 0, j // 2)

            def body(r):
                b, q = r.b, r.q
                if r.tail_only:
                    evac_rows(r.t("X", 0), 0)
                    evac_rows(r.t("X", 1), 1)
                    router_exp(b - 1)
                    return
                stages = not (isinstance(b, int) and b + 2 >= B)
                for j in range(KV_HEADS):
                    if not r.last:
                        evac_q(r.t("Q", j), 1 - q, j)
                    if j > 1:
                        evac_o(b, j - 2)
                    if j:
                        exps(b, j, 0)
                    if not r.last:
                        evac_k(r.t("K", j), 1 - q, j)
                    if not j:
                        exps(b, j, 0)
                    exps(b, j, 1)
                    if stages and j and j % 2 == 0:
                        stage_hi(b + 2, q, r.m + 1, j // 2 - 1)
                    if not r.first:
                        if j == 2:
                            evac_rows(r.t("X", 0), 0)
                        if j == 3:
                            evac_rows(r.t("X", 1), 1)
                        if j == 4:
                            router_exp(b - 1)
                evac_o(b, KV_HEADS - 2)
                if stages:
                    stage_hi(b + 2, q, r.m + 1, GROUPS - 1)
                evac_o(b, KV_HEADS - 1)

            rounds(act, body)

            def split_gu_hi(e):
                act.wait_ge(w_ready, e + 1)
                act.copy(of_slot(gu_hi, e, GU_W), of_slot(w_gu, e, GU_W)).then_inc(gu_hi_ready, 1)

            def split_dn_hi(e):
                act.copy(of_slot(dn_hi, e, WD_W), of_slot(w_dn, e, WD_W)).then_inc(dn_hi_ready, 1)

            def rows_hi(i):
                act.wait_ge(xt_full, i + 1)
                wait(act, gu_full, i)
                act.copy(xT_hi[:, :], xT_ps[:, :]).then_inc(xhi_ready, 1)

            def silu(i, p):
                act.wait_ge(gu_full, i + 1)
                act.activation(silu_g[:, bass.ds(p * I, I)], s_max_both[:, bass.ds(p * (2 * S), I)],
                               ACT.Silu).then_inc(silu_ready, 1)

            def tile(i, next_expert=None):
                p, other = act.snap(i & 1), act.snap((i + 1) & 1)
                if next_expert is not None:
                    split_gu_hi(next_expert)
                silu(i + 1, other)
                rows_hi(i + 2)
                if next_expert is not None:
                    split_dn_hi(next_expert)
                act.wait_ge(y_open, i + 1)
                act.wait_ge(y_full, i + 1)
                act.copy(y_both[:, bass.ds(p * D, D)], s_exp_both[:, bass.ds(p * (G * S), D)]).then_inc(y_free, 1)

            act.sem_inc(y_free, 2)
            act.activation(silu_g[:, 0:1], gates[:, 0:1], ACT.Silu)
            split_gu_hi(0)
            split_dn_hi(0)
            act.wait_ge(lists_ready, 1)
            rows_hi(0)
            rows_hi(1)
            silu(0, 0)
            tiles_of_experts(act, tile)

        @block.vector
        def _(dve):
            steps = [0]
            base = [0]

            def step(ins):
                ins.then_inc(dve_step, 1)
                steps[0] += 1

            def settle(held=False):
                wait(dve, dve_step, base[0] + steps[0])
                if held:
                    hold(dve, dve_step)
                    steps[0] += 1

            def broadcast(ap, n):
                return ap.unsqueeze(2).to_broadcast([ap.shape[0], ap.shape[1], n])

            dve.wait_ge(consts, 19)
            dve.tensor_copy(ident_r[:, :], ident[:, :]).then_inc(gates_ready, 1)
            dve.memset(counts[:, :], 0.0)
            dve.wait_ge(gates_ready, 2)
            for c in range(DC):
                wait(dve, t_full, c + 1)
                dve.tensor_copy(router_T[:, c, :], t_ps[:, 0:E]).then_inc(t_free, 1)

            def normalise(jobs):
                cols = SC * len(jobs)
                for n, (src, *_) in enumerate(jobs):
                    for c in range(SC):
                        step(dve.bn_stats(stats[:, n * SC + c, :], src[:, c, :]))
                settle(True)
                for c in range(cols):
                    step(dve.bn_aggr(mean_var[:, c, :], stats[:, c, :]))
                settle()
                ve, vh, rs, sq, hb = (t[:, 0:cols] for t in (var_eps, var_half, rstd, root_sq, half_bits))
                step(dve.tensor_scalar(ve, mean_var[:, 0:cols, 1], EPS, None, ALU.add))
                settle()
                step(dve.tensor_scalar(hb, ve.bitcast(I32), 1, None, ALU.logical_shift_right))
                step(dve.tensor_scalar(vh, ve, -0.5, None, ALU.mult))
                settle()
                step(dve.tensor_scalar(rs.bitcast(I32), hb, -1.0, ROOT_BITS, ALU.mult, ALU.add))
                settle()
                for _ in range(NEWTON):
                    step(dve.tensor_tensor(sq, rs, rs, ALU.mult))
                    settle()
                    step(dve.tensor_tensor(sq, sq, vh, ALU.mult))
                    settle()
                    step(dve.scalar_tensor_tensor(out=rs, in0=sq, scalar=1.5, in1=rs, op0=ALU.add, op1=ALU.mult))
                    settle()
                for n, (src, dst, ready, free) in enumerate(jobs):
                    wait(dve, *free)
                    for c in range(SC):
                        at = n * SC + c
                        dve.tensor_scalar(dst[:, c, 0:D], src[:, c, :], mean_var[:, at, 0:1], rstd[:, at:at + 1],
                                          ALU.subtract, ALU.mult).then_inc(ready, 1)

            def norm_x(b, q, m):
                wait(dve, x_loaded[q], m * 32 + 32)
                return x_in[q], xn, xn_ready, (staged, b * GROUPS)

            def take_max(b, j):
                for c in range(SC):
                    for i in range(2):
                        u = 2 * c + i
                        wait(dve, smax_full, b * (4 * KV_HEADS) + (4 * j + u + 1))
                        dve.tensor_reduce(maxima[:, c, 4 * j + 2 * i:4 * j + 2 * i + 2],
                                          s_max[u % 2][:, :].rearrange("p (a s) -> p a s", a=2), AX.X,
                                          ALU.max).then_inc(smax_free, 1)

            def split_max(b):
                wait(dve, smax_free, (b + 1) * (4 * KV_HEADS))
                step(dve.tensor_copy(max_parts[:, :, 0:HEADS], maxima[:, :, :]))
                settle()
                dve.tensor_tensor(max_parts[:, :, HEADS:], maxima[:, :, :], max_parts[:, :, 0:HEADS].bitcast(F32),
                                  ALU.subtract).then_inc(max_ready, 1)

            def evac_max(b, t):
                wait(dve, t_full, t + 1)
                wait(dve, max_rows, b * 64)
                dve.tensor_copy(maxT[:, :], t_ps[0:2 * HEADS, 0:S]).then_inc(t_free, 1)

            def divide(t, j):
                wait(dve, t_full, t + 1)
                o = t_ps[:, :].rearrange("p (n w) -> p n w", w=32)
                step(dve.reciprocal(recip[:, :].unsqueeze(2), o[:, :, DH:DH + 1]))
                settle()
                rc = recip[:, :].rearrange("p (c n) -> p c n", c=SC).unsqueeze(3).to_broadcast([P, SC, 2 * G, DH])
                dst = attn[:, :, j * G * DH:(j + 2) * G * DH].rearrange("p c (n d) -> p c n d", d=DH)
                dve.tensor_tensor(dst, o[:, :, 0:DH].rearrange("p (c n) d -> p c n d", c=SC), rc,
                                  ALU.mult).then_inc(t_free, 1)
                steps.append(0)

            def residual(b, q, m):
                wait(dve, res_loaded[q], m * 16 + 16)
                wait(dve, x1_stored[q], m * 16 + 16)
                wait(dve, t_free, last_divide[0])
                dve.scalar_tensor_tensor(out=x1[q][:, :, :], in0=attn[:, :, :], scalar=gates[:, 0:1],
                                         in1=x_res[q][:, :, :], op0=ALU.mult, op1=ALU.add).then_inc(x1_ready, 1)
                wait(dve, x1_ready, b + 1)
                return x1[q], rows_sb[q], rows_ready, (rows_stored[q], m * 16 + 16)

            def route(b, q, t):
                wait(dve, t_full, t + 1)
                lg = t_ps[:, 0:SC * E].rearrange("p (c e) -> p c e", c=SC)
                step(dve.tensor_reduce(row2[:, 0, :], lg, AX.X, ALU.max))
                settle()
                dve.tensor_tensor(logits[:, :, :], lg, broadcast(row2[:, 0, :], E), ALU.subtract).then_inc(t_free, 1)
                wait(dve, t_free, t + 1)
                dve.sem_inc(shifted, 1)

            def route_top(b, q):
                wait(dve, expd_ready, b + 1)
                step(dve.tensor_reduce(row2[:, 1, :], expd[:, :, :], AX.X, ALU.add))
                settle()
                step(dve.reciprocal(row2[:, 3, :], row2[:, 1, :]))
                settle()
                step(dve.tensor_tensor(pr[:, :, :], expd[:, :, :], broadcast(row2[:, 3, :], E), ALU.mult))
                settle(True)
                for c in range(SC):
                    step(dve.max(top[:, c, :], pr[:, c, :]))
                settle(True)
                for c in range(SC):
                    step(dve.match_replace(out=zapped[:, c, :], in_to_replace=top[:, c, :], in_values=pr[:, c, :],
                                           imm_value=-1.0))
                step(dve.tensor_reduce(row2[:, 2, :], top[:, :, :], AX.X, ALU.add))
                settle()
                step(dve.tensor_scalar(mask[:, :, :], zapped[:, :, :], 0.0, None, ALU.is_lt))
                dve.tensor_scalar(mask_bf[:, :, :], zapped[:, :, :], 0.0, None, ALU.is_lt).then_inc(mask_ready, 1)
                settle()
                step(dve.scalar_tensor_tensor(out=weighted[:, :, :], in0=pr[:, :, :], scalar=gates[:, 1:2],
                                              in1=mask[:, :, :], op0=ALU.mult, op1=ALU.mult))
                step(dve.reciprocal(row2[:, 0, :], row2[:, 2, :]))
                settle()
                dve.tensor_tensor(rows_sb[q][:, :, D:], weighted[:, :, :], broadcast(row2[:, 0, :], E),
                                  ALU.mult).then_inc(w_rows, 1)

            def find_places(b, q, t):
                wait(dve, t_full, t + 1)
                cb = counts[:, :].unsqueeze(1).to_broadcast([P, SC, E])
                step(dve.tensor_tensor(rank[:, :, :], t_ps[:, 0:SC * E].rearrange("p (c e) -> p c e", c=SC), cb, ALU.add))
                settle()
                dve.tensor_tensor(counts[:, :], counts[:, :], t_ps[:, SC * E:(SC + 1) * E], ALU.add).then_inc(t_free, 1)
                settle()
                step(dve.tensor_copy(rank_i[:, :, :], rank[:, :, :]))
                settle()
                step(dve.tensor_scalar(in_tile[:, :, :], rank_i[:, :, :], P - 1, COL_BITS, ALU.bitwise_and,
                                       ALU.logical_shift_left))
                step(dve.tensor_scalar(rank_i[:, :, :], rank_i[:, :, :], P_BITS, None, ALU.logical_shift_right))
                settle()
                step(dve.tensor_tensor(key[:, :, :], in_tile[:, :, :], rank_i[:, :, :], ALU.add))
                settle()
                step(dve.tensor_tensor(key[:, :, :], key[:, :, :], col_base[:, :, :], ALU.add))
                settle()
                step(dve.tensor_tensor(key[:, :, :], key[:, :, :], mask[:, :, :], ALU.mult))
                settle(True)
                for c in range(SC):
                    step(dve.max(top[:, c, :], key[:, c, :]))
                settle()
                wait(dve, place_free, b + 1)
                dve.tensor_scalar(place[q][:, :], top[:, :, :].rearrange("p c k -> p (c k)"), -1.0, None, ALU.add)
                step(dve.tensor_copy(token_i[q][:, :], token[:, :]))
                settle()
                dve.tensor_scalar(token[:, :], token[:, :], float(S), None, ALU.add).then_inc(place_ready, 1)

            last_divide = [0]
            normalise([norm_x(0, 0, 0)])
            normalise([norm_x(1, 1, 0)])
            for j in range(KV_HEADS):
                take_max(0, j)
            split_max(0)
            evac_max(0, T_START + 2 * KV_HEADS)

            def body(r):
                b, q = r.b, r.q
                jobs = []
                if not r.first:
                    last_divide[0] = r.t0
                    jobs.append(residual(b - 1, 1 - q, (r.m if q == 1 else r.m - 1)))
                if not (isinstance(b, int) and b + 2 >= B):
                    jobs.append(norm_x(b + 2, q, r.m + 1))
                normalise(jobs)
                if r.tail_only:
                    route(b - 1, 1 - q, r.t("L"))
                    route_top(b - 1, 1 - q)
                    find_places(b - 1, 1 - q, r.t("R"))
                    return
                for j in range(KV_HEADS):
                    if j and not r.last:
                        take_max(b + 1, j - 1)
                    if j >= 3 and j % 2:
                        divide(r.t("O", j - 3), j - 3)
                    if not r.first:
                        if j == 4:
                            route(b - 1, 1 - q, r.t("L"))
                        if j == 5:
                            route_top(b - 1, 1 - q)
                        if j == 7:
                            find_places(b - 1, 1 - q, r.t("R"))
                if not r.last:
                    take_max(b + 1, KV_HEADS - 1)
                    split_max(b + 1)
                    evac_max(b + 1, r.t("M"))
                divide(r.t("O", KV_HEADS - 2), KV_HEADS - 2)

            def stretch(r):
                steps[0] = 0
                body(r)
                return steps[0]

            base[0] = steps[0]
            base[0] += stretch(Round(0, 0))
            before = base[0]
            PER = DVE_STEPS
            with dve.Fori(0, (B - 4) // 2) as n:
                base[0] = n * (2 * PER) + before
                got = stretch(Round(2 * n + 1, 1, n))
                base[0] = n * (2 * PER) + (before + got)
                got2 = stretch(Round(2 * n + 2, 0, n + 1))
                assert got == got2 == PER, (got, got2)
            base[0] = before + (B - 4) * PER
            for b in range(B - 3, B + 1):
                base[0] += stretch(Round(b, b % 2))
            steps[0] = 0

            dve.wait_ge(place_ready, B)
            step(dve.tensor_scalar(n_tiles[:, :], counts[:, :], P - 1.0, None, ALU.add))
            settle()
            step(dve.tensor_copy(whole[:, :], n_tiles[:, :]))
            settle()
            step(dve.tensor_scalar(whole[:, :], whole[:, :], P_BITS, None, ALU.logical_shift_right))
            settle()
            step(dve.tensor_scalar(n_tiles[:, :], whole[:, :], float(MIN_TILES), None, ALU.max))
            settle()
            step(dve.memset(started[:, :], 1.0))
            settle()
            step(dve.tensor_tensor_scan(tile_end[:, :], started[:, :], n_tiles[:, :], 0.0, ALU.mult, ALU.add))
            settle()
            for c in range(2):
                step(dve.tensor_scalar(started[:, :], tile_end[:, :], tile_no[:, c:c + 1], None, ALU.is_le))
                settle()
                step(dve.tensor_reduce(tile_vals[:, c, 1:2], started[:, :], AX.X, ALU.add))
                step(dve.tensor_tensor(started[:, :], started[:, :], n_tiles[:, :], ALU.mult))
                settle()
                step(dve.tensor_reduce(tile_vals[:, c, 2:3], started[:, :], AX.X, ALU.add))
                settle()
                step(dve.tensor_tensor(tile_vals[:, c, 3:4], tile_no[:, c:c + 1], tile_vals[:, c, 2:3], ALU.subtract))
                settle()
                step(dve.scalar_tensor_tensor(out=tile_vals[:, c, 0:1], in0=tile_vals[:, c, 1:2], scalar=float(PLACES),
                                              in1=tile_vals[:, c, 3:4], op0=ALU.mult, op1=ALU.add))
                settle()
                step(dve.tensor_scalar(tile_vals[:, c, 0:1], tile_vals[:, c, 0:1], float(COLS), None, ALU.min))
                step(dve.tensor_scalar(tile_vals[:, c, 1:2], tile_vals[:, c, 1:2], E - 1.0, None, ALU.min))
                settle()
            dve.sem_inc(vals_ready, 1)
            step(dve.memset(lists[0:1, LIST_START:LIST_START + 1], 0))
            step(dve.tensor_copy(lists[0:1, LIST_START + 1:LIST_START + E], tile_end[0:1, 0:E - 1]))
            step(dve.tensor_scalar(whole[0:1, 0:1], tile_end[0:1, E - 1:E], 1.0, None, ALU.add))
            settle()
            step(dve.tensor_scalar(lists[0:1, LIST_PAIRS:LIST_PAIRS + 1], whole[0:1, 0:1], 1, None,
                                   ALU.logical_shift_right))
            step(dve.tensor_scalar(lists[0:1, LIST_START + E:LIST_START + E + 1], whole[0:1, 0:1], 1, 1,
                                   ALU.logical_shift_right, ALU.logical_shift_left))
            dve.wait_ge(lists_ps, 1)
            step(dve.tensor_copy(lists[0:1, 0:512], t_ps[0:1, 0:512]))
            settle()
            dve.sem_inc(lists_ready, 1)

            def expert_of(i):
                at = slice(LIST_E + i, LIST_E + i + 1) if isinstance(i, int) else bass.ds(i + LIST_E, 1)
                return dve.value_load(lists[0:1, at], min_val=0, max_val=E - 1)

            def split_gu_lo(e):
                dve.wait_ge(gu_hi_ready, e + 1)
                dve.tensor_tensor(of_slot(gu_lo, e, GU_W), of_slot(w_gu, e, GU_W),
                                  of_slot(gu_hi, e, GU_W).bitcast(F32), ALU.subtract).then_inc(gu_split, 1)

            def split_dn_lo(e):
                dve.wait_ge(dn_hi_ready, e + 1)
                dve.tensor_tensor(of_slot(dn_lo, e, WD_W), of_slot(w_dn, e, WD_W),
                                  of_slot(dn_hi, e, WD_W).bitcast(F32), ALU.subtract).then_inc(dn_split, 1)

            def rows_lo(i, p):
                e = expert_of(i)
                dve.wait_ge(xhi_ready, i + 1)
                dve.tensor_tensor(xT_lo[:, :], xT_ps[:, :], xT_hi[:, :].bitcast(F32), ALU.subtract).then_inc(xt_ready, 1)
                dve.tensor_copy(w_tok[:, bass.ds(p, 1)],
                                x_in_both[:, bass.ds(p * (SC * D) + (e + D), 1)]).then_inc(wtok_ready, 1)

            def hidden(i, p):
                dve.wait_ge(wtok_ready, i + 1)
                dve.wait_ge(silu_ready, i + 1)
                dve.scalar_tensor_tensor(out=h_both[:, bass.ds(p * I, I)], in0=silu_g[:, bass.ds(p * I, I)],
                                         scalar=w_tok[:, bass.ds(p, 1)],
                                         in1=s_max_both[:, bass.ds(p * (2 * S) + I, I)],
                                         op0=ALU.mult, op1=ALU.mult).then_inc(h_ready, 1)

            def tile(i, next_expert=None):
                p, other = dve.snap(i & 1), dve.snap((i + 1) & 1)
                dve.wait_ge(ht_full, i + 1)
                dve.tensor_copy(hT_hi[:, :], hT_ps[0:IH, 0:2 * P]).then_inc(hthi_ready, 1)
                dve.wait_ge(hthi_ready, i + 1)
                dve.tensor_tensor(hT_lo[:, :], hT_ps[0:IH, 0:2 * P], hT_hi[:, :].bitcast(F32),
                                  ALU.subtract).then_inc(ht_ready, 1)
                if next_expert is not None:
                    split_gu_lo(next_expert)
                rows_lo(i + 2, p)
                hidden(i + 1, other)
                if next_expert is not None:
                    split_dn_lo(next_expert)

            split_gu_lo(0)
            split_dn_lo(0)
            rows_lo(0, 0)
            rows_lo(1, 1)
            hidden(0, 0)
            tiles_of_experts(dve, tile)

            for n in range(PIECES):
                dve.wait_ge(sum_in[n], 32)
                dve.tensor_tensor(addend(0, n), addend(0, n), addend(1, n), ALU.add).then_inc(summed, 1)


DVE_STEPS = 52

_INS = ["x", "ctx_512", "g_xattn", "g_ffn", "L0_ffn_router_w", "L0_ffn_w_gate", "L0_ffn_w_up", "L0_ffn_w_down"]
_OUT = ((8, 256, 512), "float32")


def kernel(**inputs):
    import numpy as np
    import concourse.bacc as bacc
    from concourse.bass_utils import run_bass_kernel_spmd

    nc = bacc.Bacc("TRN2", target_bir_lowering=False, num_devices=1)
    arrays, args = {}, []
    for name in _INS:
        a = np.ascontiguousarray(inputs[name])
        arrays[f"in_{name}"] = a
        args.append(nc.dram_tensor(f"in_{name}", a.shape, mybir.dt.from_np(a.dtype), kind="ExternalInput").ap())
    args.append(nc.dram_tensor("out_0", _OUT[0], mybir.dt.from_np(np.dtype(_OUT[1])), kind="ExternalOutput").ap())
    flamingo_block(nc, *args)
    r = run_bass_kernel_spmd(nc, [arrays], core_ids=[0])
    return r.results[0]["out_0"]
```

```python
from contextlib import ExitStack

import concourse.bass as bass
from concourse import mybir

F32 = mybir.dt.float32
F32R = mybir.dt.float32r
BF16 = mybir.dt.bfloat16
I32 = mybir.dt.int32
U32 = mybir.dt.uint32
ALU = mybir.AluOpType
ACT = mybir.ActivationFunctionType
AX = mybir.AxisListType

P = 128
HEADS, KV_HEADS = 32, 8
TOP_K = 8
EPS = 1e-5
ROOT_BITS = float(0x5F3759DF)
NEWTON = 3


def flamingo_block(nc, x, ctx, g_xattn, g_ffn, router_w, w_gate, w_up, w_down, out):
    B, S, D = x.shape
    E, _, I = w_gate.shape
    DH = D // HEADS
    G = HEADS // KV_HEADS
    SC = S // P
    DC = D // P
    T = B * S
    SPARE = T
    ROWS = T + 2 * P
    XW = D + E
    PLACES = T // P
    COLS = E * PLACES
    IH = I // 2
    GU_W, WD_W = DC * 2 * I, 2 * D
    STK = 4 * DH
    PAIRS = HEADS // 2
    GROUPS = KV_HEADS // 2
    GH = HEADS // GROUPS
    MIN_TILES = 3
    MAX_TILES = T * TOP_K // P + MIN_TILES * E
    COPIES = 8
    P_BITS, COL_BITS = P.bit_length() - 1, COLS.bit_length() - 1
    assert D == 512 and SC == 2 and B == 8 and STK == 64 and G == 4 and E == 32

    with ExitStack() as stack:
        def sb(name, shape, dt=F32):
            return stack.enter_context(nc.sbuf_tensor(name, shape, dt))

        def psum(name, shape):
            return stack.enter_context(nc.psum_tensor(name, shape, F32))

        def sem(name):
            return stack.enter_context(nc.semaphore(name))

        def two(make, name, *args):
            return [make(f"{name}{i}", *args) for i in range(2)]

        rows_d = nc.dram_tensor("expert_rows", [ROWS, XW], F32, kind="Internal").ap()
        places_d = nc.dram_tensor("places", [P * COLS, 1], I32, kind="Internal").ap()
        acc_d = nc.dram_tensor("acc", [ROWS, D], F32, kind="Internal").ap()

        ident = sb("ident", [P, P])
        ident_r = sb("ident_r", [P, P], F32R)
        earlier = sb("earlier", [P, P], BF16)
        ones = sb("ones", [P, P], BF16)
        zeros = sb("zeros", [P, XW])
        first_place = sb("first_place", [P, E])
        tile_no = sb("tile_no", [P, 2])
        gates = sb("gates", [P, 2])
        gates_in = sb("gates_in", [P, 2])
        router_sb = sb("router_sb", [E, D])
        router_T = sb("router_T", [P, DC, E])

        x_in_both = sb("x_in", [P, 2 * SC * D])
        x_in = [x_in_both[:, i * SC * D:(i + 1) * SC * D].rearrange("p (c d) -> p c d", c=SC) for i in range(2)]
        ctx_in = two(sb, "ctx_in", [P, SC, KV_HEADS * DH])
        x_res = two(sb, "x_res", [P, SC, D])
        stats = sb("stats", [P, 2 * SC, 6])
        mean_var = sb("mean_var", [P, 2 * SC, 2])
        rstd = sb("rstd", [P, 2 * SC])
        var_eps = sb("var_eps", [P, 2 * SC]); var_half = sb("var_half", [P, 2 * SC])
        root_sq = sb("root_sq", [P, 2 * SC])
        half_bits = sb("half_bits", [P, 2 * SC], I32)
        xn = sb("xn", [P, SC, D])
        q_stage = sb("q_stage", [P, SC, HEADS * STK], F32R)
        k_stage = sb("k_stage", [P, SC, STK + KV_HEADS * 2 * STK], F32R)
        v_aug = two(sb, "v_aug", [P, SC, KV_HEADS, 32])
        qT = two(sb, "qT", [P, PAIRS, S], F32R)
        kT = two(sb, "kT", [P, KV_HEADS, 2, S], F32R)
        maxima = sb("maxima", [P, SC, HEADS])
        max_parts = sb("max_parts", [P, SC, 2 * HEADS], F32R)
        maxT = sb("maxT", [2 * HEADS, S], F32R)
        probs = two(sb, "probs", [P, SC, G * S])
        oT = two(sb, "oT", [P, S])
        recip = sb("recip", [P, 4 * G])
        attn = sb("attn", [P, GROUPS, SC * GH * DH])
        x1 = two(sb, "x1", [P, SC, D])
        rows_sb = two(sb, "rows_sb", [P, SC, XW])
        xnT = sb("xnT", [P, SC, D])
        logits = sb("logits", [P, SC, E])
        expd = sb("expd", [P, SC, E])
        row2 = sb("row2", [P, 4, SC])
        pr = sb("pr", [P, SC, E])
        top = sb("top", [P, SC, TOP_K])
        zapped = sb("zapped", [P, SC, E])
        mask = sb("mask", [P, SC, E])
        mask_bf = sb("mask_bf", [P, SC, E], BF16)
        weighted = sb("weighted", [P, SC, E])
        counts = sb("counts", [P, E])
        rank = sb("rank", [P, SC, E])
        rank_i = sb("rank_i", [P, SC, E], I32)
        in_tile = sb("in_tile", [P, SC, E], I32)
        key = sb("key", [P, SC, E])
        place = two(sb, "place", [P, SC * TOP_K], I32)
        token = sb("token", [P, SC])
        token_i = two(sb, "token_i", [P, SC], I32)

        n_tiles = sb("n_tiles", [P, E])
        tile_end = sb("tile_end", [P, E])
        started = sb("started", [P, E])
        whole = sb("whole", [P, E], I32)
        tile_vals = sb("tile_vals", [P, 2, 4])
        LIST_E, LIST_FIRST, LIST_START, LIST_PAIRS = 256, 512, 768, 768 + E + 1
        lists = sb("lists", [1, LIST_PAIRS + 1], I32)
        assert MAX_TILES + 4 <= LIST_E
        token_of = sb("token_of", [P, COLS + 1], I32)
        gather_idx = two(sb, "gather_idx", [P, 1], I32)
        add_idx = two(sb, "add_idx", [P, 1], I32)
        xg = [x_in[i][:, :, :].rearrange("p c d -> p (c d)")[:, 0:XW] for i in range(2)]
        w_tok = sb("w_tok", [P, 2])
        silu_g = sb("silu_g", [P, 2 * I])
        h_both = sb("h", [P, 2 * I])
        y_both = sb("y", [P, 2 * D])
        h = [h_both[:, i * I:(i + 1) * I] for i in range(2)]
        y = [y_both[:, i * D:(i + 1) * D] for i in range(2)]
        xT_hi = sb("xT_hi", [P, D], F32R); xT_lo = sb("xT_lo", [P, D], F32R)
        hT_hi = sb("hT_hi", [IH, 2 * P], F32R); hT_lo = sb("hT_lo", [IH, 2 * P], F32R)
        w_gu = sb("w_gu", [P, 2 * GU_W])
        w_dn = sb("w_dn", [IH, 2 * WD_W])
        gu_hi, gu_lo = (t[:, :, :].rearrange("p a s -> p (a s)") for t in qT)
        dn_hi, dn_lo = (t[0:IH, :, :, :].rearrange("p a c s -> p (a c s)") for t in kT)

        s_max_both = psum("s_max", [P, 4 * S])
        s_max = [s_max_both[:, i * 2 * S:(i + 1) * 2 * S] for i in range(2)]
        s_exp_both = psum("s_exp", [P, 4 * S])
        s_exp = [s_exp_both[:, i * 2 * S:(i + 1) * 2 * S] for i in range(2)]
        o_ps = psum("o_ps", [P, 512])
        tq_ps = psum("tq_ps", [P, 512])
        tk_ps = psum("tk_ps", [P, 512])
        t_ps = psum("t_ps", [P, 512])
        tq_psr, tk_psr, t_psr = (t[:, :].bitcast(F32R) for t in (tq_ps, tk_ps, t_ps))
        gu_ps, hT_ps, xT_ps = s_max, o_ps, t_ps
        y_ps = [s_exp[i][:, 0:D] for i in range(2)]

        consts = sem("consts"); consts_in = sem("consts_in");
        gates_ready = sem("gates_ready")
        N_FILLS = 17
        N_CONSTS = N_FILLS + 6
        x_loaded = two(sem, "x_loaded"); res_loaded = two(sem, "res_loaded")
        xn_ready = sem("xn_ready"); hi_ready = sem("hi_ready"); staged = sem("staged"); v_copied = sem("v_copied")
        pool_hold = sem("pool_hold")
        dve_step = sem("dve_step"); pe_hold = sem("pe_hold"); place_free = sem("place_free")
        t_full = sem("t_full"); t_free = sem("t_free")
        tq_full = sem("tq_full"); tq_free = sem("tq_free"); tk_full = sem("tk_full"); tk_free = sem("tk_free")
        smax_full = sem("smax_full"); smax_free = sem("smax_free")
        sexp_full = sem("sexp_full"); sexp_free = sem("sexp_free")
        o_full = sem("o_full"); o_free = sem("o_free")
        max_ready = sem("max_ready"); max_rows = sem("max_rows")
        attn_ready = sem("attn_ready"); x1_ready = sem("x1_ready"); rows_ready = sem("rows_ready"); w_rows = sem("w_rows")
        x1_stored = two(sem, "x1_stored"); rows_stored = two(sem, "rows_stored")
        shifted = sem("shifted"); expd_ready = sem("expd_ready"); mask_ready = sem("mask_ready")
        place_ready = sem("place_ready"); token_sent = sem("token_sent")
        vals_ready = sem("vals_ready"); lists_ps = sem("lists_ps"); lists_ready = sem("lists_ready")
        places_back = sem("places_back")
        w_in = sem("w_in"); w_ready = sem("w_ready")
        gu_hi_ready = sem("gu_hi_ready"); dn_hi_ready = sem("dn_hi_ready")
        gu_split = sem("gu_split"); dn_split = sem("dn_split")
        xhi_ready = sem("xhi_ready"); hthi_ready = sem("hthi_ready"); y_open = sem("y_open")
        x_got = two(sem, "x_got"); y_sent = two(sem, "y_sent")
        xt_full = sem("xt_full"); xt_ready = sem("xt_ready"); wtok_ready = sem("wtok_ready")
        gu_full = sem("gu_full"); silu_ready = sem("silu_ready"); h_ready = sem("h_ready")
        ht_full = sem("ht_full"); ht_ready = sem("ht_ready")
        y_full = sem("y_full"); y_free = sem("y_free"); idx_ready = sem("idx_ready")
        moe_done = sem("moe_done")
        out_done = sem("out_done")

        def wait(eng, s, value):
            if not isinstance(value, int) or value > 0:
                eng.wait_ge(s, value)

        def hold(eng, s):
            eng.sem_inc(s, 1)

        def uses_of_round(first, last, tail_only=False):
            order = []
            if not tail_only:
                for j in range(KV_HEADS):
                    if j >= 3 and j % 2:
                        order.append(("O", j - 3))
                    if not first:
                        order += {3: [("X", 0)], 4: [("X", 1)], 5: [("L", 0)], 7: [("R", 0)]}.get(j, [])
                if not last:
                    order.append(("M", 0))
                order.append(("O", KV_HEADS - 2))
            else:
                order = [("X", 0), ("X", 1), ("L", 0), ("R", 0)]
            return {u: n for n, u in enumerate(order)}

        T_START = 1
        T_PRE = T_START + 1
        U_FIRST = uses_of_round(True, False)
        U_MID = uses_of_round(False, False)
        U_LAST = uses_of_round(False, True)
        U_TAIL = uses_of_round(False, False, True)
        N_FIRST, N_MID, N_LAST = len(U_FIRST), len(U_MID), len(U_LAST)

        class Round:

            def __init__(self, b, q, m=None):
                self.b, self.q = b, q
                self.m = m if m is not None else b // 2
                self.first = isinstance(b, int) and b == 0
                self.last = isinstance(b, int) and b == B - 1
                self.tail_only = isinstance(b, int) and b == B
                self.uses = U_FIRST if self.first else U_LAST if self.last else U_TAIL if self.tail_only else U_MID
                if self.first:
                    self.t0 = T_PRE
                elif self.tail_only:
                    self.t0 = T_PRE + N_FIRST + (B - 2) * N_MID + N_LAST
                else:
                    self.t0 = (b - 1) * N_MID + (T_PRE + N_FIRST)

            def t(self, kind, j=0):
                return self.t0 + self.uses[(kind, j)]

        def rounds(eng, body):
            body(Round(0, 0))
            with eng.Fori(0, (B - 4) // 2) as n:
                body(Round(2 * n + 1, 1, n))
                body(Round(2 * n + 2, 0, n + 1))
            for b in range(B - 3, B + 1):
                body(Round(b, b % 2))

        batch_rows = "(c p) d -> p c d"
        SCORE_SCALE = float(DH) ** -0.5

        def tiles_of_experts(eng, tile):
            start = eng.alloc_register("first_tile")
            eng.reg_mov(start, 0)

            def expert(e, first_splits, last_splits):
                first = eng.snap(start, min_val=0, max_val=MAX_TILES)
                tile(first, first_splits, None)
                at = slice(LIST_START + e + 1, LIST_START + e + 2) if isinstance(e, int) else bass.ds(e + LIST_START + 1, 1)
                end = eng.value_load(lists[0:1, at], min_val=0, max_val=MAX_TILES)
                eng.reg_mov(start, end)
                with eng.Fori(first + 1, end - 1) as i:
                    tile(i)
                last = eng.snap(start, min_val=0, max_val=MAX_TILES) - 1
                tile(last, None, last_splits)

            with eng.Fori(0, E - 2) as e:
                expert(e, e + 1, e + 2)
            expert(E - 2, E - 1, None)
            expert(E - 1, None, None)

        def of_slot(t, e, width):
            return t[:, bass.ds((e & 1) * width, width)]

        def q_part(g, part):
            stacks = q_stage[:, :, g * GH * STK:(g + 1) * GH * STK].rearrange("p c (h w) -> p c h w", w=STK)
            return stacks[:, :, :, part * DH:(part + 1) * DH]

        def k_part(g, part):
            stacks = k_stage[:, :, STK + g * 4 * STK:STK + (g + 1) * 4 * STK].rearrange("p c (k w) -> p c k w", w=2 * STK)
            return stacks[:, :, :, part * DH:(part + 1) * DH]

        def xn_heads(g):
            return xn[:, :, g * GH * DH:(g + 1) * GH * DH].rearrange("p c (h w) -> p c h w", w=DH)

        def ctx_heads(q, g):
            return ctx_in[q][:, :, g * 2 * DH:(g + 1) * 2 * DH].rearrange("p c (k w) -> p c k w", w=DH)

        block = stack.enter_context(nc.Block())

        @block.sync
        def _(sp):
            def cut(t, b, n):
                return t[bass.ds(b * S, n * S), :] if not isinstance(b, int) else t[b * S:(b + n) * S, :]

            xf = x.rearrange("b s d -> (b s) d")
            cf = ctx.rearrange("b s d -> (b s) d")

            def load_x(b, q):
                sp.dma_start(x_in[q][:, :, :], cut(xf, b, 1).rearrange(batch_rows, p=P)).then_inc(x_loaded[q], 16)
                sp.dma_start(ctx_in[q][:, :, :], cut(cf, b, 1).rearrange(batch_rows, p=P)).then_inc(x_loaded[q], 16)

            def load_res(b, q):
                sp.dma_start(x_res[q][:, :, :], cut(xf, b, 1).rearrange(batch_rows, p=P)).then_inc(res_loaded[q], 16)

            def insert_max(b, q):
                wait(sp, t_free, b)
                for half in range(2):
                    for part in range(2):
                        at = STK * half + 3 * DH + part
                        sp.dma_start(qT[q][at:at + 1, :, :].bitcast(F32),
                                     maxT[HEADS * part + half:HEADS * (part + 1):2, :].bitcast(F32)).then_inc(max_rows, 16)

            load_x(0, 0)
            sp.dma_start(router_sb[:, :], router_w).then_inc(consts_in, 16)
            sp.dma_start(gates_in[:, 0:1], g_xattn.partition_broadcast(P)).then_inc(consts_in, 16)
            sp.dma_start(gates_in[:, 1:2], g_ffn.partition_broadcast(P)).then_inc(consts_in, 16)
            load_x(1, 1)
            load_res(0, 0)
            sp.wait_ge(consts, 1)
            part = 2 * P // 4
            for n, stored in enumerate(x1_stored + rows_stored):
                sp.dma_start(rows_d[SPARE + n * part:SPARE + (n + 1) * part, :], zeros[0:part, :]).then_inc(stored, 16)

            def load_after(b, q):
                wait(sp, staged, (b - 1) * GROUPS)
                wait(sp, v_copied, b - 1)
                load_x(b, q)

            load_after(2, 0)
            insert_max(T_PRE, 0)

            def body(r):
                b, q = r.b, r.q
                if not r.first:
                    wait(sp, x1_ready, b * GROUPS)
                    sp.dma_start(cut(acc_d, b - 1, 1).rearrange(batch_rows, p=P),
                                 x1[1 - q][:, :, :]).then_inc(x1_stored[1 - q], 16)
                if not r.tail_only and not r.last:
                    load_res(b + 1, 1 - q)
                if not (isinstance(b, int) and b + 3 >= B):
                    load_after(b + 3, 1 - q)
                if not r.first:
                    wait(sp, w_rows, b)
                    sp.dma_start(cut(rows_d, b - 1, 1).rearrange(batch_rows, p=P),
                                 rows_sb[1 - q][:, :, :]).then_inc(rows_stored[1 - q], 16)
                if not r.tail_only and not r.last:
                    insert_max(r.t("M") + 1, 1 - q)

            rounds(sp, body)

            def load_expert(e, slot):
                one = (slice(e, e + 1) if isinstance(e, int) else bass.ds(e, 1))
                gu = w_gu[:, slot * GU_W:(slot + 1) * GU_W].rearrange("p (c n) -> p c n", c=DC)
                for n, w in enumerate((w_gate, w_up)):
                    sp.dma_start(gu[:, :, n * I:(n + 1) * I],
                                 w[one].rearrange("o (c p) i -> p (o c) i", p=P)).then_inc(w_in, 16)
                sp.dma_start(w_dn[:, slot * WD_W:(slot + 1) * WD_W].rearrange("p (c n) -> p c n", c=2),
                             w_down[one].rearrange("o (c p) n -> p (o c) n", p=IH)).then_inc(w_in, 16)
                sp.wait_ge(w_in, (e + 1) * 48)
                sp.sem_inc(w_ready, 1)

            load_expert(0, 0)
            load_expert(1, 1)
            with sp.Fori(1, E // 2) as n:
                for slot in range(2):
                    sp.wait_ge(gu_split, n * 2 + (slot - 1))
                    sp.wait_ge(dn_split, n * 2 + (slot - 1))
                    load_expert(n * 2 + slot, slot)

            sp.wait_ge(moe_done, 1)
            out_rows = out.rearrange("b s d -> (b s) d")
            for n in range(COPIES):
                rows = slice(n * T // COPIES, (n + 1) * T // COPIES)
                sp.dma_start(out_rows[rows, :], acc_d[rows, :]).then_inc(out_done, 16)
            sp.wait_ge(out_done, COPIES * 16)

        @block.gpsimd
        def _(pool):
            pool.memset(zeros[:, :], 0.0).then_inc(consts, 1)
            pool.iota(token_of[:, 0:COLS].rearrange("p (c o) -> p c o", o=2), pattern=[[0, COLS // 2], [P, 2]],
                      base=SPARE, channel_multiplier=1).then_inc(consts, 1)
            pool.iota(token_of[:, COLS:], pattern=[[0, 1]], base=SPARE, channel_multiplier=1).then_inc(consts, 1)
            pool.memset(ident[:, :], 0.0).then_inc(consts, 1)
            pool.memset(earlier[:, :], 1.0).then_inc(consts, 1)
            pool.memset(ones[:, :], 1.0).then_inc(consts, 1)
            for c in range(SC):
                stacks = q_stage[:, c, :].bitcast(F32).rearrange("p (h w) -> p h w", w=STK)
                pool.memset(stacks[:, :, 3 * DH:], 0.0).then_inc(consts, 1)
                pool.memset(k_stage[:, c, 0:STK].bitcast(F32), 0.0).then_inc(consts, 1)
                stacks = k_stage[:, c, STK:].bitcast(F32).rearrange("p (k w) -> p k w", w=2 * STK)
                pool.memset(stacks[:, :, 3 * DH:], 0.0).then_inc(consts, 1)
            pool.memset(v_aug[0][:, :, :, :], 0.0).then_inc(consts, 1)
            pool.memset(v_aug[1][:, :, :, :], 0.0).then_inc(consts, 1)
            pool.iota(first_place[:, :], pattern=[[PLACES * P, E]], base=0, channel_multiplier=0,
                      allow_small_or_imprecise_dtypes=True).then_inc(consts, 1)
            pool.iota(tile_no[:, :], pattern=[[P, 2]], base=0, channel_multiplier=1,
                      allow_small_or_imprecise_dtypes=True).then_inc(consts, 1)
            pool.iota(token[:, :], pattern=[[P, SC]], base=0, channel_multiplier=1,
                      allow_small_or_imprecise_dtypes=True).then_inc(consts, 1)
            pool.wait_ge(consts, N_FILLS)
            pool.affine_select(out=ident[:, :], in_=ident[:, :], compare_op=ALU.not_equal, fill=1.0, base=0,
                               pattern=[[-1, P]], channel_multiplier=1).then_inc(consts, 1)
            pool.affine_select(out=earlier[:, :], in_=earlier[:, :], compare_op=ALU.is_gt, fill=0.0, base=0,
                               pattern=[[1, P]], channel_multiplier=-1).then_inc(consts, 1)
            for c in range(SC):
                kk = k_stage[:, c, STK:].bitcast(F32).rearrange("p (k w) -> p k w", w=2 * STK)
                pool.memset(kk[:, :, 3 * DH:3 * DH + 2], -1.0).then_inc(consts, 1)
            for q in range(2):
                pool.memset(v_aug[q][:, :, :, DH:DH + 1], 1.0).then_inc(consts, 1)
            pool.wait_ge(consts, N_CONSTS)


            def stage_lo(b, q, m, g):
                wait(pool, hi_ready, b * GROUPS + (g + 1))
                pool.tensor_tensor(q_part(g, 1), xn_heads(g), q_part(g, 0).bitcast(F32), ALU.subtract)
                pool.tensor_tensor(k_part(g, 2), ctx_heads(q, g), k_part(g, 0).bitcast(F32),
                                   ALU.subtract).then_inc(staged, 1)

            def copy_v(b, q, m):
                wait(pool, x_loaded[q], m * 32 + 32)
                wait(pool, o_full, (b - 1) * KV_HEADS)
                hold(pool, pool_hold)
                for c in range(SC):
                    i = pool.tensor_copy(v_aug[q][:, c, :, 0:DH],
                                         ctx_in[q][:, c, :].rearrange("p (k w) -> p k w", w=DH))
                i.then_inc(v_copied, 1)

            def add_x(b, q, m, g):
                if g == 0:
                    wait(pool, res_loaded[q], m * 16 + 16)
                    wait(pool, x1_stored[q], m * 16 + 16)
                    wait(pool, rows_ready, (b - 1) * SC)
                wait(pool, attn_ready, b * GROUPS + (g + 1))
                cols = slice(g * GH * DH, (g + 1) * GH * DH)
                pool.tensor_tensor(x1[q][:, :, cols], attn[:, g, :].rearrange("p (c n) -> p c n", c=SC),
                                   x_res[q][:, :, cols], ALU.add).then_inc(x1_ready, 1)

            def scatter(b, q, at_once):
                if at_once.start == 0:
                    if not (isinstance(b, int) and b == B - 1):
                        wait(pool, token_sent, b * (SC * TOP_K * 16) + 16)
                        pool.sem_inc(place_free, 1)
                    wait(pool, place_ready, b + 1)
                    hold(pool, pool_hold)
                for at in at_once:
                    c = at // TOP_K
                    pool.indirect_dma_start(places_d, bass.IndirectOffsetOnAxis(place[q][:, at:at + 1].bitcast(U32), 0),
                                            token_i[q][:, c:c + 1], None).then_inc(token_sent, 16)

            pool.sem_inc(place_free, 1)
            for g in range(GROUPS):
                stage_lo(0, 0, 0, g)
            copy_v(0, 0, 0)
            for g in range(GROUPS):
                stage_lo(1, 1, 0, g)
            def body(r):
                b, q = r.b, r.q
                if not (r.last or r.tail_only):
                    copy_v(b + 1, 1 - q, (r.m if q == 0 else r.m + 1))
                per = SC * TOP_K // GROUPS
                for g in range(GROUPS):
                    if not (isinstance(b, int) and b < 2):
                        scatter(b - 2, q, range(g * per, (g + 1) * per))
                    if not (isinstance(b, int) and b + 2 >= B):
                        stage_lo(b + 2, q, r.m + 1, g)
                    if not r.tail_only:
                        add_x(b, q, r.m, g)

            pool.dma_start(places_d.rearrange("(p c) o -> p (c o)", p=P), token_of[:, 0:COLS]).then_inc(token_sent, 16)
            for a in range(2):
                spare = slice(SPARE + a * P, SPARE + (a + 1) * P)
                pool.dma_start(acc_d[spare, :], zeros[:, 0:D]).then_inc(y_sent[a], 16)
            body(Round(0, 0))
            body(Round(1, 1))
            with pool.Fori(0, (B - 4) // 2) as n:
                body(Round(2 * n + 2, 0, n + 1))
                body(Round(2 * n + 3, 1, n + 1))
            for b in range(B - 2, B + 1):
                body(Round(b, b % 2))
            scatter(B - 1, (B - 1) % 2, range(SC * TOP_K))

            pool.wait_ge(token_sent, T // P * TOP_K * 16 + 16)
            pool.dma_start(token_of[:, 0:COLS], places_d.rearrange("(p c) o -> p (c o)", p=P)).then_inc(places_back, 16)
            pool.wait_ge(places_back, 16)
            for q in range(2):
                pool.wait_ge(rows_stored[q], 16 * B // 2 + 16)
                pool.wait_ge(x1_stored[q], 16 * B // 2 + 16)
            pool.wait_ge(lists_ready, 1)

            def column(i):
                at = slice(i, i + 1) if isinstance(i, int) else bass.ds(i, 1)
                col = pool.value_load(lists[0:1, at], min_val=0, max_val=COLS)
                return token_of[:, bass.ds(col, 1)]

            def gather(i, p, count):
                pool.tensor_copy(gather_idx[p][:, :], column(i)).then_inc(idx_ready, 1)
                pool.wait_ge(idx_ready, count + 1)
                hold(pool, idx_ready)
                pool.indirect_dma_start(xg[p], None, rows_d,
                                        bass.IndirectOffsetOnAxis(gather_idx[p][:, 0:1].bitcast(U32), 0)).then_inc(x_got[p], 16)

            def add_rows(i, p, n, count):
                pool.tensor_copy(add_idx[p][:, :], column(i)).then_inc(idx_ready, 1)
                pool.wait_ge(idx_ready, count + 1)
                pool.wait_ge(y_free, i + 3)
                first = pool.value_load(lists[0:1, bass.ds(i + LIST_FIRST, 1)], min_val=0, max_val=MAX_TILES)
                pool.wait_ge(y_sent[0], ((first + 1) >> 1) * 16 + 16)
                pool.wait_ge(y_sent[1], (first >> 1) * 16 + 16)
                hold(pool, idx_ready)
                pool.indirect_dma_start(acc_d, bass.IndirectOffsetOnAxis(add_idx[p][:, 0:1].bitcast(U32), 0),
                                        y[p][:, :], None, compute_op=ALU.add).then_inc(y_sent[p], 16)

            gather(0, 0, 0)
            gather(1, 1, 2)
            for i in range(2):
                pool.wait_ge(xt_full, i + 1)
                pool.wait_ge(wtok_ready, i + 1)
                gather(i + 2, i, 4 + 2 * i)
            pairs = pool.value_load(lists[0:1, LIST_PAIRS:LIST_PAIRS + 1], min_val=1, max_val=MAX_TILES // 2)
            with pool.Fori(0, pairs) as n:
                for p in range(2):
                    i = n * 2 + p
                    count = n * 10 + (8 + 5 * p)
                    pool.wait_ge(y_sent[p], n * 16 + 16)
                    pool.sem_inc(y_open, 1)
                    pool.wait_ge(xt_full, i + 3)
                    pool.wait_ge(wtok_ready, i + 3)
                    hold(pool, idx_ready)
                    gather(i + 4, p, count + 1)
                    add_rows(i, p, n, count + 3)
            for p in range(2):
                pool.wait_ge(y_sent[p], pairs * 16 + 16)
                pool.wait_ge(x_got[p], pairs * 16 + 32)
            pool.sem_inc(moe_done, 1)

        @block.tensor
        def _(pe):
            pe.wait_ge(consts, N_CONSTS)
            pe.wait_ge(consts_in, 48)
            for c in range(DC):
                m = pe.transpose(t_ps[:, c * E:(c + 1) * E], router_sb[:, c * P:(c + 1) * P], ident[0:E, 0:E])
            m.then_inc(t_full, 1)
            pe.wait_ge(gates_ready, 2)

            def transpose_q(b, j):
                wait(pe, tq_free, b * KV_HEADS + j)
                for i in range(2):
                    for c in range(SC):
                        m = pe.transpose(tq_psr[:, (i * SC + c) * P:(i * SC + c + 1) * P],
                                         q_stage[:, c, (2 * j + i) * P:(2 * j + i + 1) * P], ident_r[:, :])
                m.then_inc(tq_full, 1)

            def transpose_k(b, j):
                wait(pe, tk_free, b * KV_HEADS + j)
                for half in range(2):
                    for c in range(SC):
                        at = 2 * STK * j + (STK if half == 0 else 0)
                        m = pe.transpose(tk_psr[:, (half * SC + c) * P:(half * SC + c + 1) * P],
                                         k_stage[:, c, at:at + P], ident_r[:, :])
                m.then_inc(tk_full, 1)

            def first_scores(j):
                wait(pe, tq_free, j + 1)
                wait(pe, tk_free, j + 1)
                for u in range(4):
                    c, i = u // 2, u % 2
                    wait(pe, smax_free, 4 * (j - 1) + u + 1)
                    for half in range(2):
                        m = pe.matmul((s_max + s_exp)[u][:, half * S:(half + 1) * S],
                                      qT[0][:, 2 * j + i, c * P:(c + 1) * P], kT[0][:, j, half, :],
                                      start=True, stop=True)
                    m.then_inc(smax_full, 1)

            def scores_for_max(b, q, j, parts):
                wait(pe, tq_free, b * KV_HEADS + (j + 1))
                wait(pe, tk_free, b * KV_HEADS + (j + 1))
                for u in parts:
                    c, i = u // 2, u % 2
                    wait(pe, smax_free, b * (4 * KV_HEADS) + (4 * j + u - 1))
                    for half in range(2):
                        m = pe.matmul(s_max[u % 2][:, half * S:(half + 1) * S],
                                      qT[q][:, 2 * j + i, c * P:(c + 1) * P], kT[q][:, j, half, :],
                                      start=True, stop=True)
                    m.then_inc(smax_full, 1)

            def transpose_max(b, t):
                wait(pe, t_free, t)
                wait(pe, max_ready, b + 1)
                hold(pe, pe_hold)
                for c in range(SC):
                    m = pe.transpose(t_psr[0:2 * HEADS, c * P:(c + 1) * P], max_parts[:, c, :], ident_r[:, :])
                m.then_inc(t_full, 1)

            def scores_for_exp(b, q, j, u):
                c, half = u // 2, u % 2
                wait(pe, sexp_free, b * (4 * KV_HEADS) + (4 * j + u + 1))
                pe.matmul(s_exp[half], kT[q][:, j, half, c * P:(c + 1) * P], qT[q][:, 2 * j:2 * j + 2, :],
                          start=True, stop=True).then_inc(sexp_full, 1)

            def values(b, q, j):
                wait(pe, o_free, b * KV_HEADS + j)
                for c in range(SC):
                    wait(pe, sexp_free, b * (4 * KV_HEADS) + (4 * j + 2 * c + 4))
                    for half in range(2):
                        for i in range(2):
                            g = 2 * i + half
                            at = (2 * half + i) * S
                            m = pe.matmul(o_ps[32 * g:32 * g + 32, 0:S], v_aug[q][:, c, j, :],
                                          probs[j % 2][:, c, at:at + S], start=(c == 0), stop=(c == SC - 1),
                                          tile_position=(0, 32 * g))
                m.then_inc(o_full, 1)

            def transpose_o(b, t, j):
                wait(pe, t_free, t)
                wait(pe, o_free, b * KV_HEADS + (j + 2))
                for c in range(SC):
                    for i in range(2):
                        m = pe.transpose(t_ps[:, (2 * c + i) * P:(2 * c + i + 1) * P],
                                         oT[i][:, c * P:(c + 1) * P], ident[:, :])
                m.then_inc(t_full, 1)

            def transpose_rows(b, q, t, c):
                wait(pe, rows_ready, (b + 1) * SC)
                wait(pe, t_free, t)
                for n in range(DC):
                    m = pe.transpose(t_ps[:, n * P:(n + 1) * P], rows_sb[q][:, c, n * P:(n + 1) * P], ident[:, :])
                m.then_inc(t_full, 1)

            def router_logits(t):
                wait(pe, t_free, t)
                for c in range(SC):
                    for n in range(DC):
                        m = pe.matmul(t_ps[:, c * E:(c + 1) * E], xnT[:, c, n * P:(n + 1) * P], router_T[:, n, :],
                                      start=(n == 0), stop=(n == DC - 1))
                m.then_inc(t_full, 1)

            def ranks(b, t):
                wait(pe, t_free, t)
                wait(pe, mask_ready, b + 1)
                pe.matmul(t_ps[:, 0:E], earlier[:, :], mask_bf[:, 0, :], start=True, stop=True)
                pe.matmul(t_ps[:, E:2 * E], earlier[:, :], mask_bf[:, 1, :], start=True, stop=False)
                pe.matmul(t_ps[:, E:2 * E], ones[:, :], mask_bf[:, 0, :], start=False, stop=True)
                pe.matmul(t_ps[:, 2 * E:3 * E], ones[:, :], mask_bf[:, 0, :], start=True, stop=False)
                pe.matmul(t_ps[:, 2 * E:3 * E], ones[:, :], mask_bf[:, 1, :], start=False, stop=True).then_inc(t_full, 1)

            for j in range(KV_HEADS):
                pe.wait_ge(staged, j // 2 + 1)
                transpose_q(0, j)
                transpose_k(0, j)
                if j:
                    first_scores(j - 1)
            first_scores(KV_HEADS - 1)
            transpose_max(0, T_START)

            def body(r):
                b, q = r.b, r.q
                if r.tail_only:
                    transpose_rows(b - 1, 1 - q, r.t("X", 0), 0)
                    transpose_rows(b - 1, 1 - q, r.t("X", 1), 1)
                    router_logits(r.t("L"))
                    ranks(b - 1, r.t("R"))
                    return

                def next_max(j, parts):
                    if j >= 0 and not r.last:
                        scores_for_max(b + 1, 1 - q, j, parts)

                def next_stacks(j, transpose):
                    if j < KV_HEADS and not r.last:
                        wait(pe, staged, (b + 1) * GROUPS + (j // 2 + 1))
                        transpose(b + 1, j)

                for j in range(KV_HEADS):
                    if j == 0:
                        next_stacks(0, transpose_q)
                        next_stacks(0, transpose_k)
                        next_stacks(1, transpose_q)
                        next_stacks(1, transpose_k)
                        wait(pe, max_rows, (b + 1) * 64)
                    else:
                        next_stacks(j + 1, transpose_q)
                    next_max(j - 1, (0,))
                    next_max(j - 1, (1,))
                    scores_for_exp(b, q, j, 0)
                    scores_for_exp(b, q, j, 1)
                    if j:
                        next_stacks(j + 1, transpose_k)
                    next_max(j - 1, (2,))
                    scores_for_exp(b, q, j, 2)
                    next_max(j - 1, (3,))
                    if j >= 3 and j % 2:
                        transpose_o(b, r.t("O", j - 3), j - 3)
                    if j == 1:
                        wait(pe, v_copied, b + 1)
                    scores_for_exp(b, q, j, 3)
                    if j:
                        values(b, q, j - 1)
                    if not r.first:
                        if j == 3:
                            transpose_rows(b - 1, 1 - q, r.t("X", 0), 0)
                        if j == 4:
                            transpose_rows(b - 1, 1 - q, r.t("X", 1), 1)
                        if j == 5:
                            router_logits(r.t("L"))
                        if j == 7:
                            ranks(b - 1, r.t("R"))
                next_max(KV_HEADS - 1, range(4))
                values(b, q, KV_HEADS - 1)
                if not r.last:
                    transpose_max(b + 1, r.t("M"))
                transpose_o(b, r.t("O", KV_HEADS - 2), KV_HEADS - 2)

            rounds(pe, body)

            t_b = T_PRE + N_FIRST + (B - 2) * N_MID + N_LAST + len(U_TAIL)
            pe.wait_ge(vals_ready, 1)
            pe.wait_ge(t_free, t_b)
            for n in range(2):
                for c in range(2):
                    m = pe.matmul(t_ps[0:1, (2 * n + c) * P:(2 * n + c + 1) * P], tile_vals[:, c, n:n + 1],
                                  ident[:, :], start=True, stop=True)
            for c in range(2):
                m = pe.matmul(o_ps[0:1, c * P:(c + 1) * P], tile_vals[:, c, 2:3], ident[:, :], start=True, stop=True)
            m.then_inc(lists_ps, 1)
            pe.wait_ge(lists_ready, 1)

            def transpose_x(i, p, n):
                pe.wait_ge(x_got[p], n * 16 + 16)
                for c in range(DC):
                    m = pe.transpose(xT_ps[:, c * P:(c + 1) * P], xg[p][:, c * P:(c + 1) * P], ident[:, :])
                m.then_inc(xt_full, 1)

            def expert_of(i):
                at = slice(LIST_E + i, LIST_E + i + 1) if isinstance(i, int) else bass.ds(i + LIST_E, 1)
                return pe.value_load(lists[0:1, at], min_val=0, max_val=E - 1)

            def transpose_h(i, p):
                pe.wait_ge(h_ready, i + 1)
                for c in range(2):
                    m = pe.transpose(hT_ps[0:IH, c * P:(c + 1) * P], h[p][:, c * IH:(c + 1) * IH], ident[:, :])
                m.then_inc(ht_full, 1)

            def gate_up(i, p, e, between=None):
                off = pe.snap((e & 1) * GU_W)
                pe.wait_ge(gu_split, e + 1)
                pe.wait_ge(xhi_ready, i + 1)
                for c in range(DC):
                    for w in (gu_hi, gu_lo):
                        pe.matmul(gu_ps[p][:, 0:2 * I], xT_hi[:, c * P:(c + 1) * P],
                                  w[:, c * 2 * I:c * 2 * I + GU_W + 2 * I][:, bass.ds(off, 2 * I)],
                                  start=(c == 0 and w is gu_hi), stop=False)
                if between:
                    between()
                pe.wait_ge(xt_ready, i + 1)
                for c in range(DC):
                    m = pe.matmul(gu_ps[p][:, 0:2 * I], xT_lo[:, c * P:(c + 1) * P],
                                  gu_hi[:, c * 2 * I:c * 2 * I + GU_W + 2 * I][:, bass.ds(off, 2 * I)],
                                  start=False, stop=(c == DC - 1))
                m.then_inc(gu_full, 1)

            def down(i, p, e):
                off = pe.snap((e & 1) * WD_W)
                pe.wait_ge(dn_split, e + 1)
                pe.wait_ge(hthi_ready, i + 1)
                pe.wait_ge(y_free, i + 1)
                for c in range(2):
                    for w in (dn_hi, dn_lo):
                        pe.matmul(y_ps[p], hT_hi[:, c * P:(c + 1) * P], w[:, c * D:c * D + WD_W + D][:, bass.ds(off, D)],
                                  start=(c == 0 and w is dn_hi), stop=False)
                pe.wait_ge(ht_ready, i + 1)
                for c in range(2):
                    m = pe.matmul(y_ps[p], hT_lo[:, c * P:(c + 1) * P], dn_hi[:, c * D:c * D + WD_W + D][:, bass.ds(off, D)],
                                  start=False, stop=(c == 1))
                m.then_inc(y_full, 1)

            transpose_x(0, 0, 0)
            pe.wait_ge(xt_ready, 1)
            transpose_x(1, 1, 0)
            gate_up(0, 0, 0)
            pairs = pe.value_load(lists[0:1, LIST_PAIRS:LIST_PAIRS + 1], min_val=1, max_val=MAX_TILES // 2)
            carried = [pe.alloc_register(f"expert_of_next{k}") for k in range(2)]
            for k in range(2):
                pe.reg_mov(carried[k], expert_of(k))
            with pe.Fori(0, pairs) as n:
                e = [pe.snap(reg, min_val=0, max_val=E - 1) for reg in carried]
                for p in range(2):
                    i = n * 2 + p
                    gate_up(i + 1, 1 - p, e[p + 1], lambda i=i, p=p: transpose_h(i, p))
                    transpose_x(i + 2, p, n + 1)
                    e.append(expert_of(i + 2))
                    down(i, p, e[p])
                for k in range(2):
                    pe.reg_mov(carried[k], e[k + 2])

        @block.scalar
        def _(act):
            act.wait_ge(consts_in, 48)
            act.activation(gates[:, :], gates_in[:, :], ACT.Tanh).then_inc(gates_ready, 1)
            act.sem_inc(sexp_free, 2)

            def stage_hi(b, q, m, g):
                wait(act, x_loaded[q], m * 32 + 32)
                wait(act, xn_ready, (b + 1) * SC)
                for part in (0, 2):
                    act.copy(q_part(g, part), xn_heads(g))
                for part in (0, 1):
                    i = act.copy(k_part(g, part), ctx_heads(q, g))
                i.then_inc(hi_ready, 1)

            def evac_q(b, q, j):
                wait(act, tq_full, b * KV_HEADS + (j + 1))
                act.copy(qT[q][:, 2 * j:2 * j + 2, :].rearrange("p a s -> p (a s)"), tq_ps[:, :]).then_inc(tq_free, 1)

            def evac_k(b, q, j):
                wait(act, tk_full, b * KV_HEADS + (j + 1))
                act.copy(kT[q][:, j, :, :].rearrange("p a s -> p (a s)"), tk_ps[:, :]).then_inc(tk_free, 1)

            def exps(b, j, u):
                c, half = u // 2, u % 2
                wait(act, o_full, b * KV_HEADS + (j - 1))
                wait(act, sexp_full, b * (4 * KV_HEADS) + (4 * j + u + 1))
                act.activation(probs[j % 2][:, c, half * 2 * S:(half + 1) * 2 * S], s_exp[half], ACT.Exp,
                               scale=SCORE_SCALE).then_inc(sexp_free, 1)

            def evac_o(b, j):
                wait(act, o_full, b * KV_HEADS + (j + 1))
                act.copy(oT[j % 2][:, :], o_ps[:, 0:S]).then_inc(o_free, 1)

            def evac_rows(t, c):
                wait(act, t_full, t + 1)
                act.copy(xnT[:, c, :], t_ps[:, :]).then_inc(t_free, 1)

            def router_exp(b):
                wait(act, shifted, b + 1)
                act.activation(expd[:, :, :], logits[:, :, :], ACT.Exp).then_inc(expd_ready, 1)

            for g in range(GROUPS):
                stage_hi(0, 0, 0, g)
            for j in range(KV_HEADS):
                evac_q(0, 0, j)
                evac_k(0, 0, j)
                if j % 2:
                    stage_hi(1, 1, 0, j // 2)

            def body(r):
                b, q = r.b, r.q
                if r.tail_only:
                    evac_rows(r.t("X", 0), 0)
                    evac_rows(r.t("X", 1), 1)
                    router_exp(b - 1)
                    return
                stages = not (isinstance(b, int) and b + 2 >= B)
                for j in range(KV_HEADS):
                    if not r.last:
                        for jj in ((0, 1) if j == 0 else (j + 1,)):
                            if jj < KV_HEADS:
                                evac_q(b + 1, 1 - q, jj)
                            if j == 0:
                                evac_k(b + 1, 1 - q, jj)
                    if j > 1:
                        evac_o(b, j - 2)
                    exps(b, j, 0)
                    exps(b, j, 1)
                    if not r.first and j == 6:
                        router_exp(b - 1)
                    if 0 < j < KV_HEADS - 1 and not r.last:
                        evac_k(b + 1, 1 - q, j + 1)
                    exps(b, j, 2)
                    exps(b, j, 3)
                    if stages and j >= 3 and j % 2:
                        stage_hi(b + 2, q, r.m + 1, (j - 3) // 2)
                    if not r.first:
                        if j == 3:
                            evac_rows(r.t("X", 0), 0)
                        if j == 4:
                            evac_rows(r.t("X", 1), 1)
                evac_o(b, KV_HEADS - 2)
                if stages:
                    stage_hi(b + 2, q, r.m + 1, GROUPS - 1)
                evac_o(b, KV_HEADS - 1)

            rounds(act, body)

            def split_gu_hi(e):
                act.wait_ge(w_ready, e + 1)
                act.copy(of_slot(gu_hi, e, GU_W), of_slot(w_gu, e, GU_W)).then_inc(gu_hi_ready, 1)

            def split_dn_hi(e):
                act.copy(of_slot(dn_hi, e, WD_W), of_slot(w_dn, e, WD_W)).then_inc(dn_hi_ready, 1)

            def rows_hi(i):
                act.wait_ge(xt_full, i + 1)
                wait(act, gu_full, i)
                act.copy(xT_hi[:, :], xT_ps[:, :]).then_inc(xhi_ready, 1)

            def silu(i, p):
                act.wait_ge(gu_full, i + 1)
                act.activation(silu_g[:, bass.ds(p * I, I)], s_max_both[:, bass.ds(p * (2 * S), I)],
                               ACT.Silu).then_inc(silu_ready, 1)

            def tile(i, first_splits=None, last_splits=None):
                p, other = act.snap(i & 1), act.snap((i + 1) & 1)
                silu(i + 1, other)
                rows_hi(i + 2)
                if first_splits is not None:
                    split_dn_hi(first_splits)
                if last_splits is not None:
                    split_gu_hi(last_splits)
                act.wait_ge(y_open, i + 1)
                act.wait_ge(y_full, i + 1)
                act.copy(y_both[:, bass.ds(p * D, D)], s_exp_both[:, bass.ds(p * (2 * S), D)]).then_inc(y_free, 1)

            act.sem_inc(y_free, 2)
            act.activation(silu_g[:, 0:1], gates[:, 0:1], ACT.Silu)
            split_gu_hi(0)
            split_dn_hi(0)
            split_gu_hi(1)
            act.wait_ge(lists_ready, 1)
            rows_hi(0)
            rows_hi(1)
            silu(0, 0)
            tiles_of_experts(act, tile)

        @block.vector
        def _(dve):
            steps = [0]
            base = [0]

            def step(ins):
                ins.then_inc(dve_step, 1)
                steps[0] += 1

            def settle(held=False):
                wait(dve, dve_step, base[0] + steps[0])
                if held:
                    hold(dve, dve_step)
                    steps[0] += 1

            def broadcast(ap, n):
                return ap.unsqueeze(2).to_broadcast([ap.shape[0], ap.shape[1], n])

            OF_X1, OF_X = 0, SC

            def take_stats(src, at):
                for c in range(SC):
                    step(dve.bn_stats(stats[:, at + c, :], src[:, c, :]))
                settle(True)
                for c in range(SC):
                    step(dve.bn_aggr(mean_var[:, at + c, :], stats[:, at + c, :]))

            def roots(start, end):
                ve, vh, rs, sq, hb = (t[:, start:end] for t in (var_eps, var_half, rstd, root_sq, half_bits))
                settle()
                step(dve.tensor_scalar(ve, mean_var[:, start:end, 1], EPS, None, ALU.add))
                settle()
                step(dve.tensor_scalar(hb, ve.bitcast(I32), 1, None, ALU.logical_shift_right))
                step(dve.tensor_scalar(vh, ve, -0.5, None, ALU.mult))
                settle()
                step(dve.tensor_scalar(rs.bitcast(I32), hb, -1.0, ROOT_BITS, ALU.mult, ALU.add))
                settle()
                for _ in range(NEWTON):
                    step(dve.tensor_tensor(sq, rs, rs, ALU.mult))
                    settle()
                    step(dve.tensor_tensor(sq, sq, vh, ALU.mult))
                    settle()
                    step(dve.scalar_tensor_tensor(out=rs, in0=sq, scalar=1.5, in1=rs, op0=ALU.add, op1=ALU.mult))
                    settle()

            def apply_norm(src, dst, at, ready):
                for c in range(SC):
                    dve.tensor_scalar(dst[:, c, 0:D], src[:, c, :], mean_var[:, at + c, 0:1], rstd[:, at + c:at + c + 1],
                                      ALU.subtract, ALU.mult).then_inc(ready, 1)

            def stats_x(b, q, m):
                wait(dve, x_loaded[q], m * 32 + 32)
                take_stats(x_in[q], OF_X)

            def norm_x(b, q):
                wait(dve, staged, b * GROUPS)
                apply_norm(x_in[q], xn, OF_X, xn_ready)

            def stats_x1(b, q):
                wait(dve, x1_ready, (b + 1) * GROUPS)
                take_stats(x1[q], OF_X1)

            def norm_x1(b, q, m):
                wait(dve, rows_stored[q], m * 16 + 16)
                apply_norm(x1[q], rows_sb[q], OF_X1, rows_ready)

            def take_max(b, j, banks=s_max):
                for c in range(SC):
                    for i in range(2):
                        u = 2 * c + i
                        wait(dve, smax_full, b * (4 * KV_HEADS) + (4 * j + u + 1))
                        dve.tensor_reduce(maxima[:, c, 4 * j + 2 * i:4 * j + 2 * i + 2],
                                          banks[u % len(banks)][:, :].rearrange("p (a s) -> p a s", a=2), AX.X,
                                          ALU.max).then_inc(smax_free, 1)

            def split_max(b):
                wait(dve, smax_free, (b + 1) * (4 * KV_HEADS))
                step(dve.tensor_copy(max_parts[:, :, 0:HEADS], maxima[:, :, :]))
                settle()
                dve.tensor_tensor(max_parts[:, :, HEADS:], maxima[:, :, :], max_parts[:, :, 0:HEADS].bitcast(F32),
                                  ALU.subtract).then_inc(max_ready, 1)

            def evac_max(b, t):
                wait(dve, t_full, t + 1)
                wait(dve, max_rows, b * 64)
                dve.tensor_copy(maxT[:, :], t_ps[0:2 * HEADS, 0:S]).then_inc(t_free, 1)

            def divide(b, t, j):
                wait(dve, t_full, t + 1)
                o = t_ps[:, :].rearrange("p (n w) -> p n w", w=32)
                step(dve.reciprocal(recip[:, :].unsqueeze(2), o[:, :, DH:DH + 1]))
                settle()
                wait(dve, x1_ready, (b - 1) * GROUPS + (j // 2 + 1))
                dve.scalar_tensor_tensor(out=attn[:, j // 2, :].rearrange("p (n d) -> p n d", d=DH),
                                         in0=o[:, :, 0:DH], scalar=gates[:, 0:1],
                                         in1=recip[:, :].unsqueeze(2).to_broadcast([P, SC * GH, DH]),
                                         op0=ALU.mult, op1=ALU.mult).then_inc(t_free, 1)
                dve.wait_ge(t_free, t + 1)
                dve.sem_inc(attn_ready, 1)

            def route(b, q, t):
                wait(dve, t_full, t + 1)
                lg = t_ps[:, 0:SC * E].rearrange("p (c e) -> p c e", c=SC)
                step(dve.tensor_reduce(row2[:, 0, :], lg, AX.X, ALU.max))
                settle()
                dve.tensor_tensor(logits[:, :, :], lg, broadcast(row2[:, 0, :], E), ALU.subtract).then_inc(t_free, 1)
                wait(dve, t_free, t + 1)
                dve.sem_inc(shifted, 1)

            def route_top(b, q):
                wait(dve, expd_ready, b + 1)
                step(dve.tensor_reduce(row2[:, 1, :], expd[:, :, :], AX.X, ALU.add))
                settle()
                step(dve.reciprocal(row2[:, 3, :], row2[:, 1, :]))
                settle()
                step(dve.tensor_tensor(pr[:, :, :], expd[:, :, :], broadcast(row2[:, 3, :], E), ALU.mult))
                settle(True)
                for c in range(SC):
                    step(dve.max(top[:, c, :], pr[:, c, :]))
                settle(True)
                for c in range(SC):
                    step(dve.match_replace(out=zapped[:, c, :], in_to_replace=top[:, c, :], in_values=pr[:, c, :],
                                           imm_value=-1.0))
                step(dve.tensor_reduce(row2[:, 2, :], top[:, :, :], AX.X, ALU.add))
                settle()
                step(dve.tensor_scalar(mask[:, :, :], zapped[:, :, :], 0.0, None, ALU.is_lt))
                dve.tensor_scalar(mask_bf[:, :, :], zapped[:, :, :], 0.0, None, ALU.is_lt).then_inc(mask_ready, 1)
                settle()
                step(dve.scalar_tensor_tensor(out=weighted[:, :, :], in0=pr[:, :, :], scalar=gates[:, 1:2],
                                              in1=mask[:, :, :], op0=ALU.mult, op1=ALU.mult))
                step(dve.reciprocal(row2[:, 0, :], row2[:, 2, :]))
                settle()
                dve.tensor_tensor(rows_sb[q][:, :, D:], weighted[:, :, :], broadcast(row2[:, 0, :], E),
                                  ALU.mult).then_inc(w_rows, 1)

            def add_ranks(b, q, t):
                wait(dve, t_full, t + 1)
                cb = counts[:, :].unsqueeze(1).to_broadcast([P, SC, E])
                step(dve.tensor_tensor(rank[:, :, :], t_ps[:, 0:SC * E].rearrange("p (c e) -> p c e", c=SC), cb, ALU.add))
                settle()
                dve.tensor_tensor(counts[:, :], counts[:, :], t_ps[:, SC * E:(SC + 1) * E], ALU.add).then_inc(t_free, 1)
                settle()

            def place_ranks(b, q):
                step(dve.tensor_copy(rank_i[:, :, :], rank[:, :, :]))
                settle()
                step(dve.tensor_scalar(in_tile[:, :, :], rank_i[:, :, :], P - 1, COL_BITS, ALU.bitwise_and,
                                       ALU.logical_shift_left))
                step(dve.tensor_scalar(rank_i[:, :, :], rank_i[:, :, :], P_BITS, None, ALU.logical_shift_right))
                settle()
                step(dve.tensor_tensor(key[:, :, :], in_tile[:, :, :], rank_i[:, :, :], ALU.add))
                settle()
                step(dve.scalar_tensor_tensor(out=key[:, :, :], in0=key[:, :, :], scalar=1.0, in1=mask[:, :, :],
                                              op0=ALU.add, op1=ALU.mult))
                settle(True)
                for c in range(SC):
                    step(dve.max(top[:, c, :], key[:, c, :]))
                settle()
                wait(dve, place_free, b + 1)
                dve.tensor_scalar(place[q][:, :], top[:, :, :].rearrange("p c k -> p (c k)"), -1.0, None, ALU.add)
                step(dve.tensor_copy(token_i[q][:, :], token[:, :]))
                settle()
                dve.tensor_scalar(token[:, :], token[:, :], float(S), None, ALU.add).then_inc(place_ready, 1)

            stats_x(0, 0, 0)
            roots(OF_X, OF_X + SC)
            norm_x(0, 0)
            dve.wait_ge(consts, N_CONSTS)
            dve.tensor_copy(ident_r[:, :], ident[:, :]).then_inc(gates_ready, 1)
            dve.tensor_copy(counts[:, :], first_place[:, :])
            dve.wait_ge(gates_ready, 2)
            dve.wait_ge(t_full, 1)
            dve.tensor_copy(router_T[:, :, :].rearrange("p c e -> p (c e)"), t_ps[:, 0:DC * E]).then_inc(t_free, 1)
            stats_x(1, 1, 0)
            roots(OF_X, OF_X + SC)
            norm_x(1, 1)
            for j in range(KV_HEADS):
                take_max(0, j, s_max + s_exp)
            split_max(0)
            evac_max(0, T_START)
            stats_x(2, 0, 1)

            def body(r):
                b, q = r.b, r.q
                prepares = not (isinstance(b, int) and b + 2 >= B)
                if not r.first:
                    stats_x1(b - 1, 1 - q)
                if prepares or not r.first:
                    roots(OF_X if r.first else OF_X1, OF_X + SC if prepares else OF_X)
                if not r.first:
                    norm_x1(b - 1, 1 - q, (r.m if q == 1 else r.m - 1))
                if r.tail_only:
                    route(b - 1, 1 - q, r.t("L"))
                    route_top(b - 1, 1 - q)
                    add_ranks(b - 1, 1 - q, r.t("R"))
                    place_ranks(b - 1, 1 - q)
                    return
                for j in range(KV_HEADS):
                    if j and not r.last:
                        take_max(b + 1, j - 1)
                    if j >= 3 and j % 2:
                        divide(b, r.t("O", j - 3), j - 3)
                    if j == 1 and prepares:
                        norm_x(b + 2, q)
                    if j == 4 and not (isinstance(b, int) and b + 3 >= B):
                        stats_x(b + 3, 1 - q, (r.m + 2 if q == 1 else r.m + 1))
                    if not r.first:
                        if j == 5:
                            route(b - 1, 1 - q, r.t("L"))
                        if j == 6:
                            route_top(b - 1, 1 - q)
                        if j == 7:
                            add_ranks(b - 1, 1 - q, r.t("R"))
                if not r.last:
                    take_max(b + 1, KV_HEADS - 1)
                    split_max(b + 1)
                    evac_max(b + 1, r.t("M"))
                divide(b, r.t("O", KV_HEADS - 2), KV_HEADS - 2)
                if not r.first:
                    place_ranks(b - 1, 1 - q)

            def stretch(r):
                steps[0] = 0
                body(r)
                return steps[0]

            base[0] = steps[0]
            base[0] += stretch(Round(0, 0))
            before = base[0]
            PER = DVE_STEPS
            with dve.Fori(0, (B - 4) // 2) as n:
                base[0] = n * (2 * PER) + before
                got = stretch(Round(2 * n + 1, 1, n))
                base[0] = n * (2 * PER) + (before + got)
                got2 = stretch(Round(2 * n + 2, 0, n + 1))
                assert got == got2 == PER, (got, got2)
            base[0] = before + (B - 4) * PER
            for b in range(B - 3, B + 1):
                base[0] += stretch(Round(b, b % 2))
            steps[0] = 0

            dve.wait_ge(place_ready, B)
            step(dve.scalar_tensor_tensor(out=n_tiles[:, :], in0=counts[:, :], scalar=P - 1.0, in1=first_place[:, :],
                                          op0=ALU.add, op1=ALU.subtract))
            settle()
            step(dve.tensor_copy(whole[:, :], n_tiles[:, :]))
            settle()
            step(dve.tensor_scalar(whole[:, :], whole[:, :], P_BITS, None, ALU.logical_shift_right))
            settle()
            step(dve.tensor_scalar(n_tiles[:, :], whole[:, :], float(MIN_TILES), None, ALU.max))
            settle()
            step(dve.memset(started[:, :], 1.0))
            settle()
            step(dve.tensor_tensor_scan(tile_end[:, :], started[:, :], n_tiles[:, :], 0.0, ALU.mult, ALU.add))
            settle()
            for c in range(2):
                step(dve.tensor_scalar(started[:, :], tile_end[:, :], tile_no[:, c:c + 1], None, ALU.is_le))
                settle()
                step(dve.tensor_reduce(tile_vals[:, c, 1:2], started[:, :], AX.X, ALU.add))
                step(dve.tensor_tensor(started[:, :], started[:, :], n_tiles[:, :], ALU.mult))
                settle()
                step(dve.tensor_reduce(tile_vals[:, c, 2:3], started[:, :], AX.X, ALU.add))
                settle()
                step(dve.tensor_tensor(tile_vals[:, c, 3:4], tile_no[:, c:c + 1], tile_vals[:, c, 2:3], ALU.subtract))
                settle()
                step(dve.scalar_tensor_tensor(out=tile_vals[:, c, 0:1], in0=tile_vals[:, c, 1:2], scalar=float(PLACES),
                                              in1=tile_vals[:, c, 3:4], op0=ALU.mult, op1=ALU.add))
                settle()
                step(dve.tensor_scalar(tile_vals[:, c, 0:1], tile_vals[:, c, 0:1], float(COLS), None, ALU.min))
                step(dve.tensor_scalar(tile_vals[:, c, 1:2], tile_vals[:, c, 1:2], E - 1.0, None, ALU.min))
                settle()
            dve.sem_inc(vals_ready, 1)
            step(dve.memset(lists[0:1, LIST_START:LIST_START + 1], 0))
            step(dve.tensor_copy(lists[0:1, LIST_START + 1:LIST_START + E], tile_end[0:1, 0:E - 1]))
            step(dve.tensor_scalar(whole[0:1, 0:1], tile_end[0:1, E - 1:E], 1.0, None, ALU.add))
            settle()
            step(dve.tensor_scalar(lists[0:1, LIST_PAIRS:LIST_PAIRS + 1], whole[0:1, 0:1], 1, None,
                                   ALU.logical_shift_right))
            step(dve.tensor_scalar(lists[0:1, LIST_START + E:LIST_START + E + 1], whole[0:1, 0:1], 1, 1,
                                   ALU.logical_shift_right, ALU.logical_shift_left))
            dve.wait_ge(lists_ps, 1)
            step(dve.tensor_copy(lists[0:1, 0:LIST_FIRST], t_ps[0:1, 0:LIST_FIRST]))
            step(dve.tensor_copy(lists[0:1, LIST_FIRST:LIST_START], o_ps[0:1, 0:2 * P]))
            settle()
            dve.sem_inc(lists_ready, 1)

            def expert_of(i):
                at = slice(LIST_E + i, LIST_E + i + 1) if isinstance(i, int) else bass.ds(i + LIST_E, 1)
                return dve.value_load(lists[0:1, at], min_val=0, max_val=E - 1)

            def split_gu_lo(e, part):
                if part == 0:
                    dve.wait_ge(gu_hi_ready, e + 1)
                lo, raw, hi = (t[:, part * GU_W // 2:][:, bass.ds((e & 1) * GU_W, GU_W // 2)] for t in (gu_lo, w_gu, gu_hi))
                i = dve.tensor_tensor(lo, raw, hi.bitcast(F32), ALU.subtract)
                if part == 1:
                    i.then_inc(gu_split, 1)

            def split_dn_lo(e):
                dve.wait_ge(dn_hi_ready, e + 1)
                dve.tensor_tensor(of_slot(dn_lo, e, WD_W), of_slot(w_dn, e, WD_W),
                                  of_slot(dn_hi, e, WD_W).bitcast(F32), ALU.subtract).then_inc(dn_split, 1)

            def rows_lo(i, p):
                e = expert_of(i)
                dve.wait_ge(xhi_ready, i + 1)
                dve.tensor_tensor(xT_lo[:, :], xT_ps[:, :], xT_hi[:, :].bitcast(F32), ALU.subtract).then_inc(xt_ready, 1)
                dve.tensor_copy(w_tok[:, bass.ds(p, 1)],
                                x_in_both[:, bass.ds(p * (SC * D) + (e + D), 1)]).then_inc(wtok_ready, 1)

            def hidden(i, p):
                dve.wait_ge(wtok_ready, i + 1)
                dve.wait_ge(silu_ready, i + 1)
                dve.scalar_tensor_tensor(out=h_both[:, bass.ds(p * I, I)], in0=silu_g[:, bass.ds(p * I, I)],
                                         scalar=w_tok[:, bass.ds(p, 1)],
                                         in1=s_max_both[:, bass.ds(p * (2 * S) + I, I)],
                                         op0=ALU.mult, op1=ALU.mult).then_inc(h_ready, 1)

            def tile(i, first_splits=None, last_splits=None):
                p, other = dve.snap(i & 1), dve.snap((i + 1) & 1)
                dve.wait_ge(ht_full, i + 1)
                dve.tensor_copy(hT_hi[:, :], hT_ps[0:IH, 0:2 * P]).then_inc(hthi_ready, 1)
                dve.wait_ge(hthi_ready, i + 1)
                dve.tensor_tensor(hT_lo[:, :], hT_ps[0:IH, 0:2 * P], hT_hi[:, :].bitcast(F32),
                                  ALU.subtract).then_inc(ht_ready, 1)
                if first_splits is not None:
                    split_gu_lo(first_splits, 1)
                rows_lo(i + 2, p)
                hidden(i + 1, other)
                if first_splits is not None:
                    split_dn_lo(first_splits)
                if last_splits is not None:
                    split_gu_lo(last_splits, 0)

            split_gu_lo(0, 0)
            split_gu_lo(0, 1)
            split_dn_lo(0)
            split_gu_lo(1, 0)
            rows_lo(0, 0)
            rows_lo(1, 1)
            hidden(0, 0)
            tiles_of_experts(dve, tile)


DVE_STEPS = 52

_INS = ["x", "ctx_512", "g_xattn", "g_ffn", "L0_ffn_router_w", "L0_ffn_w_gate", "L0_ffn_w_up", "L0_ffn_w_down"]
_OUT = ((8, 256, 512), "float32")


def kernel(**inputs):
    import numpy as np
    import concourse.bacc as bacc
    from concourse.bass_utils import run_bass_kernel_spmd

    nc = bacc.Bacc("TRN2", target_bir_lowering=False, num_devices=1)
    arrays, args = {}, []
    for name in _INS:
        a = np.ascontiguousarray(inputs[name])
        arrays[f"in_{name}"] = a
        args.append(nc.dram_tensor(f"in_{name}", a.shape, mybir.dt.from_np(a.dtype), kind="ExternalInput").ap())
    args.append(nc.dram_tensor("out_0", _OUT[0], mybir.dt.from_np(np.dtype(_OUT[1])), kind="ExternalOutput").ap())
    flamingo_block(nc, *args)
    r = run_bass_kernel_spmd(nc, [arrays], core_ids=[0])
    return r.results[0]["out_0"]
```
